# Optimizing a Trainium2 kernel written in Bass

```python
import numpy as np
import jax
import jax.numpy as jnp

def _softmax(x, axis=-1):
    return jax.nn.softmax(x, axis=axis)

def _gelu(x):
    return jax.nn.gelu(x, approximate=True)

def _silu(x):
    return jax.nn.silu(x)

def _sigmoid(x):
    return jax.nn.sigmoid(x)

def _layernorm(x, axis=-1, eps=1e-05):
    m = jnp.mean(x, axis=axis, keepdims=True)
    v = jnp.var(x, axis=axis, keepdims=True)
    return (x - m) / jnp.sqrt(v + eps)

def _scatter_add(tgt, idx, src, axis=0):
    return tgt.at[idx].add(src)

def _segment_sum(src, seg, n):
    return jax.ops.segment_sum(src, seg, n)
kernel_name = 'mk_lm_tower_d1_tok_ids256_r4_4aa2df'

def setup_inputs(seed: int=0):
    np.random.seed(seed)
    _w = jnp.asarray

    def _rec_inputs():
        import jax
        import jax.numpy as jnp
        _rk = jax.random.key(seed)
        x = jax.random.randint(jax.random.fold_in(_rk, 1), (128, 128), 0, 8000, jnp.int32)
        return x
    x = _rec_inputs()

    def _L0_tok_setup():
        import jax, jax.numpy as jnp
        import numpy as np
        VOCAB = 8000
        D = 192
        CD = 64
        B, S = (16, 512)
        N = B * S

        def _compose(src, pad_mask, wc1, bc1, wc2, bc2):
            m = pad_mask[..., None]
            mean = (src * m).sum(axis=1) / jnp.maximum(m.sum(axis=1), 1.0)
            h = jax.nn.gelu(mean @ wc1 + bc1)
            return h @ wc2 + bc2
        key = jax.random.key(seed)
        ks = jax.random.split(key, 12)
        inp = {}
        inp['chunk_input_ids'] = jax.random.randint(ks[0], (B, S), 0, VOCAB)
        inp['spans0'] = jax.random.randint(ks[1], (1024, 4), 0, 32766)
        inp['spans1'] = jax.random.randint(ks[2], (1024, 4), 0, 32766)
        inp['spans2'] = jax.random.randint(ks[3], (1024, 4), 0, 32766)
        inp['opening_nt_start_idx'] = VOCAB
        inp['emb_table'] = 0.02 * jax.random.normal(ks[4], (VOCAB, D), dtype=jnp.float32)
        inp['w_down'] = 0.02 * jax.random.normal(ks[5], (D, CD), dtype=jnp.float32)
        inp['b_down'] = jnp.zeros((CD,), dtype=jnp.float32)
        inp['wc1'] = 0.02 * jax.random.normal(ks[6], (CD, 4 * CD), dtype=jnp.float32)
        inp['bc1'] = jnp.zeros((4 * CD,), dtype=jnp.float32)
        inp['wc2'] = 0.02 * jax.random.normal(ks[7], (4 * CD, CD), dtype=jnp.float32)
        inp['bc2'] = jnp.zeros((CD,), dtype=jnp.float32)
        return inp
    _L0_tok_all = _L0_tok_setup()
    _L0_tok_in = {k: v for k, v in _L0_tok_all.items() if k in ('spans0', 'spans1', 'spans2', 'emb_table', 'w_down', 'b_down', 'wc1', 'bc1', 'wc2', 'bc2')}
    del _L0_tok_all

    def _L0_attn_setup():
        import jax, jax.numpy as jnp
        import numpy as np
        B, T, C = (16, 512, 64)
        TT = T
        LAYER_ID, N_LAYER = (3, 6)
        key = jax.random.key(seed)
        ks = jax.random.split(key, 6)
        ratio_0_to_1 = LAYER_ID / (N_LAYER - 1)
        ratio_1_to_almost0 = 1.0 - LAYER_ID / N_LAYER
        h = np.arange(TT, dtype=np.float32)
        decay_speed = -5.0 + 8.0 * (h / (TT - 1)) ** (0.7 + 1.3 * ratio_0_to_1)
        curve = -(TT - 1 - h)
        time_w = jnp.asarray(np.exp(np.clip(curve * decay_speed, -30.0, 0.0)), dtype=jnp.float32)
        i = np.arange(C, dtype=np.float32) / C
        time_mix_k = jnp.asarray((i ** ratio_1_to_almost0).reshape(1, 1, C), dtype=jnp.float32)
        time_mix_v = jnp.asarray((i ** ratio_1_to_almost0 + 0.3 * ratio_0_to_1).reshape(1, 1, C), dtype=jnp.float32)
        time_mix_r = jnp.asarray((i ** (0.5 * ratio_1_to_almost0)).reshape(1, 1, C), dtype=jnp.float32)
        x = jax.random.normal(ks[0], (B, T, C), dtype=jnp.float32)
        scale = 0.02
        Wk = scale * jax.random.normal(ks[1], (C, C), dtype=jnp.float32)
        Wv = scale * jax.random.normal(ks[2], (C, C), dtype=jnp.float32)
        Wr = scale * jax.random.normal(ks[3], (C, C), dtype=jnp.float32)
        Wo = scale * jax.random.normal(ks[4], (C, C), dtype=jnp.float32)
        return {'x': x, 'time_w': time_w, 'time_mix_k': time_mix_k, 'time_mix_v': time_mix_v, 'time_mix_r': time_mix_r, 'Wk': Wk, 'Wv': Wv, 'Wr': Wr, 'Wo': Wo}
    _L0_attn_all = _L0_attn_setup()
    _L0_attn_in = {k: v for k, v in _L0_attn_all.items() if k in ('time_w', 'time_mix_k', 'time_mix_v', 'time_mix_r', 'Wk', 'Wv', 'Wr', 'Wo')}
    del _L0_attn_all

    def _L0_ffn_setup():
        import jax, jax.numpy as jnp
        import numpy as np
        DIM = 64
        HEADS = 8
        NUM_KEYS = 64
        NUM_KV = NUM_KEYS ** 2
        PK_TOPK = 16
        FINAL_TOPK = 16
        DIM_KEY = DIM // 2
        P = 2

        def _pk(x, Wq_pk, pk_keys):
            b, n, _ = x.shape
            q = (x @ Wq_pk).reshape(b, n, P, HEADS, DIM_KEY).transpose(2, 0, 1, 3, 4)
            sim = jnp.einsum('pbnhd,pkhd->pbnhk', q, pk_keys)
            scores, idx = jax.lax.top_k(sim, PK_TOPK)
            idx0 = idx[0]
            idx1 = idx[1] * NUM_KEYS
            index = (idx0[..., :, None] + idx1[..., None, :]).reshape(b, n, HEADS, PK_TOPK * PK_TOPK)
            score = (scores[0][..., :, None] + scores[1][..., None, :]).reshape(b, n, HEADS, PK_TOPK * PK_TOPK)
            final_scores, pk_idx = jax.lax.top_k(score, FINAL_TOPK)
            final_indices = jnp.take_along_axis(index, pk_idx, axis=-1)
            final_scores = jax.nn.softmax(final_scores, axis=-1)
            return (final_scores, final_indices)
        key = jax.random.key(seed)
        ks = jax.random.split(key, 7)
        b, n = (2, 256)
        std = 0.02
        x = jax.random.normal(ks[0], (b, n, DIM), dtype=jnp.float32)
        Wq_pk = jax.random.normal(ks[1], (DIM, P * HEADS * DIM_KEY), dtype=jnp.float32) * std
        pk_keys = jax.random.normal(ks[2], (P, NUM_KEYS, HEADS, DIM_KEY), dtype=jnp.float32) * std
        Wq = jax.random.normal(ks[3], (DIM, HEADS * DIM), dtype=jnp.float32) * std
        keys_table = jax.random.normal(ks[4], (NUM_KV * HEADS, DIM), dtype=jnp.float32) * std
        values_table = jax.random.normal(ks[5], (NUM_KV * HEADS, DIM), dtype=jnp.float32) * std
        Wo = jax.random.normal(ks[6], (DIM * HEADS, DIM), dtype=jnp.float32) * std
        return {'x': x, 'Wq_pk': Wq_pk, 'pk_keys': pk_keys, 'Wq': Wq, 'keys_table': keys_table, 'values_table': values_table, 'Wo': Wo}
    _L0_ffn_all = _L0_ffn_setup()
    _L0_ffn_in = {k: v for k, v in _L0_ffn_all.items() if k in ('Wq_pk', 'pk_keys', 'Wq', 'keys_table', 'values_table', 'Wo')}
    del _L0_ffn_all
    return {'x': x, 'L0_tok_spans0': _L0_tok_in['spans0'], 'L0_tok_spans1': _L0_tok_in['spans1'], 'L0_tok_spans2': _L0_tok_in['spans2'], 'L0_tok_emb_table': _L0_tok_in['emb_table'], 'L0_tok_w_down': _L0_tok_in['w_down'], 'L0_tok_b_down': _L0_tok_in['b_down'], 'L0_tok_wc1': _L0_tok_in['wc1'], 'L0_tok_bc1': _L0_tok_in['bc1'], 'L0_tok_wc2': _L0_tok_in['wc2'], 'L0_tok_bc2': _L0_tok_in['bc2'], 'L0_attn_time_w': _L0_attn_in['time_w'], 'L0_attn_time_mix_k': _L0_attn_in['time_mix_k'], 'L0_attn_time_mix_v': _L0_attn_in['time_mix_v'], 'L0_attn_time_mix_r': _L0_attn_in['time_mix_r'], 'L0_attn_Wk': _L0_attn_in['Wk'], 'L0_attn_Wv': _L0_attn_in['Wv'], 'L0_attn_Wr': _L0_attn_in['Wr'], 'L0_attn_Wo': _L0_attn_in['Wo'], 'L0_ffn_Wq_pk': _L0_ffn_in['Wq_pk'], 'L0_ffn_pk_keys': _L0_ffn_in['pk_keys'], 'L0_ffn_Wq': _L0_ffn_in['Wq'], 'L0_ffn_keys_table': _L0_ffn_in['keys_table'], 'L0_ffn_values_table': _L0_ffn_in['values_table'], 'L0_ffn_Wo': _L0_ffn_in['Wo']}

def reference(x, L0_tok_spans0, L0_tok_spans1, L0_tok_spans2, L0_tok_emb_table, L0_tok_w_down, L0_tok_b_down, L0_tok_wc1, L0_tok_bc1, L0_tok_wc2, L0_tok_bc2, L0_attn_time_w, L0_attn_time_mix_k, L0_attn_time_mix_v, L0_attn_time_mix_r, L0_attn_Wk, L0_attn_Wv, L0_attn_Wr, L0_attn_Wo, L0_ffn_Wq_pk, L0_ffn_pk_keys, L0_ffn_Wq, L0_ffn_keys_table, L0_ffn_values_table, L0_ffn_Wo):
    import jax
    import jax.numpy as jnp

    def _L0_tok_ref(chunk_input_ids, spans0, spans1, spans2, opening_nt_start_idx, emb_table, w_down, b_down, wc1, bc1, wc2, bc2):
        import jax, jax.numpy as jnp
        import numpy as np
        VOCAB = 8000
        D = 192
        CD = 64
        B, S = (16, 512)
        N = B * S

        def _compose(src, pad_mask, wc1, bc1, wc2, bc2):
            m = pad_mask[..., None]
            mean = (src * m).sum(axis=1) / jnp.maximum(m.sum(axis=1), 1.0)
            h = jax.nn.gelu(mean @ wc1 + bc1)
            return h @ wc2 + bc2
        bsz, slen = chunk_input_ids.shape
        ids = jnp.where(chunk_input_ids == -100, 0, chunk_input_ids)
        input_embeddings = emb_table[ids]
        buf = (input_embeddings @ w_down + b_down).reshape(-1, CD)
        for spans in (spans0, spans1, spans2):
            pad_mask = (spans != -100).astype(buf.dtype)
            comp_tgt_pos = jnp.max(spans, axis=-1) + 1
            idx = jnp.where(spans == -100, 0, spans)
            comp_src = buf[idx]
            comp_out = _compose(comp_src, pad_mask, wc1, bc1, wc2, bc2)
            buf = buf.at[comp_tgt_pos].set(comp_out)
        return buf.reshape(bsz, slen, CD)

    def _L0_attn_ref(x, time_w, time_mix_k, time_mix_v, time_mix_r, Wk, Wv, Wr, Wo):
        import jax, jax.numpy as jnp
        import numpy as np
        B, T, C = (16, 512, 64)
        TT = T
        LAYER_ID, N_LAYER = (3, 6)
        Bx, Tx, Cx = x.shape
        maxlen = time_w.shape[0]
        xx = jnp.pad(x, ((0, 0), (1, 0), (0, 0)))[:, :-1]
        xk = x * time_mix_k + xx * (1.0 - time_mix_k)
        xv = x * time_mix_v + xx * (1.0 - time_mix_v)
        xr = x * time_mix_r + xx * (1.0 - time_mix_r)
        k = jnp.exp(jnp.clip(xk @ Wk, -60.0, 30.0))
        v = xv @ Wv
        r = xr @ Wr
        sum_k = jnp.cumsum(k, axis=1)
        kv = k * v
        t_idx = jnp.arange(Tx)
        d = t_idx[:, None] - t_idx[None, :]
        W = jnp.where(d >= 0, time_w[jnp.clip(maxlen - 1 - d, 0, maxlen - 1)], 0.0)
        wkv = jnp.einsum('tu,buc->btc', W, kv)
        rwkv = jax.nn.sigmoid(r) * wkv / sum_k
        return rwkv @ Wo

    def _L0_ffn_ref(x, Wq_pk, pk_keys, Wq, keys_table, values_table, Wo):
        import jax, jax.numpy as jnp
        import numpy as np
        DIM = 64
        HEADS = 8
        NUM_KEYS = 64
        NUM_KV = NUM_KEYS ** 2
        PK_TOPK = 16
        FINAL_TOPK = 16
        DIM_KEY = DIM // 2
        P = 2

        def _pk(x, Wq_pk, pk_keys):
            b, n, _ = x.shape
            q = (x @ Wq_pk).reshape(b, n, P, HEADS, DIM_KEY).transpose(2, 0, 1, 3, 4)
            sim = jnp.einsum('pbnhd,pkhd->pbnhk', q, pk_keys)
            scores, idx = jax.lax.top_k(sim, PK_TOPK)
            idx0 = idx[0]
            idx1 = idx[1] * NUM_KEYS
            index = (idx0[..., :, None] + idx1[..., None, :]).reshape(b, n, HEADS, PK_TOPK * PK_TOPK)
            score = (scores[0][..., :, None] + scores[1][..., None, :]).reshape(b, n, HEADS, PK_TOPK * PK_TOPK)
            final_scores, pk_idx = jax.lax.top_k(score, FINAL_TOPK)
            final_indices = jnp.take_along_axis(index, pk_idx, axis=-1)
            final_scores = jax.nn.softmax(final_scores, axis=-1)
            return (final_scores, final_indices)
        b, n, d = x.shape
        q = (x @ Wq).reshape(b, n, HEADS, DIM) * DIM ** (-0.5)
        kv_scores, indices = _pk(x, Wq_pk, pk_keys)
        offsets = jnp.arange(HEADS, dtype=indices.dtype) * NUM_KV
        ind = indices + offsets[None, None, :, None]
        k = jnp.einsum('bnhk,bnhkd->bnhd', kv_scores, keys_table[ind])
        v = jnp.einsum('bnhk,bnhkd->bnhd', kv_scores, values_table[ind])
        sim = jnp.einsum('bihd,bjhd->bhij', q, k)
        neg = -jnp.finfo(sim.dtype).max
        causal = jnp.tril(jnp.ones((n, n), dtype=bool))
        sim = jnp.where(causal, sim, neg)
        attn = jax.nn.softmax(sim, axis=-1)
        out = jnp.einsum('bhij,bjhd->bhid', attn, v)
        out = out.transpose(0, 2, 1, 3).reshape(b, n, HEADS * DIM)
        return out @ Wo
    h = _L0_tok_ref(x, L0_tok_spans0, L0_tok_spans1, L0_tok_spans2, 8000, L0_tok_emb_table, L0_tok_w_down, L0_tok_b_down, L0_tok_wc1, L0_tok_bc1, L0_tok_wc2, L0_tok_bc2)
    h = h + _L0_attn_ref(_layernorm(h, axis=-1), L0_attn_time_w, L0_attn_time_mix_k, L0_attn_time_mix_v, L0_attn_time_mix_r, L0_attn_Wk, L0_attn_Wv, L0_attn_Wr, L0_attn_Wo)
    h = h + _L0_ffn_ref(_layernorm(h, axis=-1), L0_ffn_Wq_pk, L0_ffn_pk_keys, L0_ffn_Wq, L0_ffn_keys_table, L0_ffn_values_table, L0_ffn_Wo)
    return h

_drawn_inputs = setup_inputs


def setup_inputs(seed=0):
    import zlib

    import numpy as np

    out = dict(_drawn_inputs(seed))
    spreads = {'L0_tok_b_down': (0.0, 0.1), 'L0_tok_bc1': (0.0, 0.435), 'L0_tok_bc2': (0.0, 0.1)}
    factors = {'L0_tok_wc1': 8.0,
     'L0_tok_wc2': 3.043,
     'L0_attn_time_mix_k': 8.0,
     'L0_attn_time_mix_v': 8.0,
     'L0_attn_time_mix_r': 8.0,
     'L0_attn_Wk': 8.0,
     'L0_attn_Wv': 4.086,
     'L0_attn_Wr': 8.0,
     'L0_attn_Wo': 3.936,
     'L0_ffn_Wq_pk': 20.501,
     'L0_ffn_Wq': 64.0,
     'L0_ffn_keys_table': 64.0,
     'L0_ffn_pk_keys': 6.118,
     'L0_ffn_values_table': 5.739,
     'L0_ffn_Wo': 5.445}
    for name, (base, spread) in spreads.items():
        noise = np.random.default_rng([zlib.crc32(name.encode()), seed]).standard_normal(out[name].shape)
        drawn = base * np.exp(spread * noise) if base else spread * noise
        out[name] = jnp.asarray(drawn.astype(out[name].dtype))
    for name, factor in factors.items():
        out[name] = (out[name] * factor).astype(out[name].dtype)
    return out
```

```python
from contextlib import ExitStack

import concourse.bass as bass
from concourse import mybir
import numpy as np

F32 = mybir.dt.float32
BF16 = mybir.dt.bfloat16
I32 = mybir.dt.int32
U32 = mybir.dt.uint32
ALU = mybir.AluOpType
ACT = mybir.ActivationFunctionType
AX = mybir.AxisListType

P = 128
B, T, C = 128, 128, 64
N_TOK = B * T
VOCAB, D_EMB = 8000, 192
N_SPAN, SPAN, ROUNDS = 1024, 4, 3
PAD = -100.0
EPS = 1e-5
HEADS, KEYS, TOPK = 8, 64, 16
NUM_KV = KEYS * KEYS
D_KEY = 32
TIME_LEN = 512
NEG = -3.0e38
MASKED = -1.0e30

BLOCK = 4
BT = BLOCK * T
UNITS = (B // BLOCK) * HEADS
CI, CJ = 16, 8
NI, NJ = KEYS // CI, KEYS // CJ
CHUNKS = NI * NJ
SLOTS = 2 * CHUNKS
SIDE0_ROWS, SIDE1_ROWS = 4 * CI, 4 * CJ
ROWS = SIDE0_ROWS + SIDE1_ROWS
SIDE_ROWS = 4 * KEYS
LOAD_UNIT = 16 * (NI + NJ + 1)

RUNS = [TOPK // (a + 1) for a in range(TOPK)]
STARTS = [sum(RUNS[:a]) for a in range(TOPK)]
PAIRS = sum(RUNS)


def wait(eng, sem, value):
    if isinstance(value, int) and value <= 0:
        return
    eng.wait_ge(sem, value)


def tower(nc, x, spans0, spans1, spans2, emb_table, w_down, b_down, wc1, bc1, wc2, bc2,
          time_w, mix_k, mix_v, mix_r, Wk, Wv, Wr, Wo, Wq_pk, pk_keys, Wq, keys_table,
          values_table, Wo_ffn, out):
    ctx = ExitStack()
    with ctx:
        def sb(name, shape, dt):
            return ctx.enter_context(nc.sbuf_tensor(name, shape, dt))

        def pb(name):
            return ctx.enter_context(nc.psum_tensor(name, [P, 512], F32))

        def sem(name):
            return ctx.enter_context(nc.semaphore(name))

        def dram(name, shape, dt):
            return nc.dram_tensor(name, shape, dt, kind="Internal").ap()

        proj_d = dram("proj_d", (VOCAB, C), F32)
        buf_d = dram("buf_d", (N_TOK, C), F32)
        tgt_d = dram("tgt_d", (ROUNDS, N_SPAN), F32)
        tw_d = dram("tw_d", (2, T), F32)
        tab_d = dram("tab_d", (HEADS, P, CHUNKS, P), F32)
        rows_d = dram("rows_d", (UNITS, 2 * SIDE_ROWS, BT), BF16)
        kv_d = dram("kv_d", (UNITS, P, BT), F32)
        h1_d = dram("h1_d", (B, T, C), F32)
        xn_d = dram("xn_d", (B, C, T), F32)

        combo_s = sb("combo_s", [P, 2 * CHUNKS * BT // 2], F32)
        table_s = sb("table_s", [P, 2 * CHUNKS * P], F32)
        hot_s = sb("hot_s", [P, 2 * HEADS * KEYS * TOPK // 2], F32)
        parts_s = sb("parts_s", [P, HEADS * 2 * SIDE_ROWS // 2], F32)
        rowsT_s = sb("rowsT_s", [P, 32 * P // 2], F32)
        combo = combo_s[:, :].bitcast(BF16).rearrange("p (k c t) -> p k c t", k=2, c=CHUNKS)
        table = table_s[:, :].rearrange("p (k c d) -> p k c d", k=2, c=CHUNKS)
        hot = hot_s[:, :].bitcast(BF16).rearrange("p (s h i a) -> p s h i a", s=2, h=HEADS, i=KEYS)
        parts = parts_s[:, :].bitcast(BF16)
        parts0 = parts.rearrange("p (h s r) -> p h s r", h=HEADS, s=2)[:, :, 0, :].rearrange(
            "p h (g q i) -> p h g q i", g=NI, q=4)
        parts1 = parts.rearrange("p (h s r) -> p h s r", h=HEADS, s=2)[:, :, 1, :].rearrange(
            "p h (g q i) -> p h g q i", g=NJ, q=4)
        rowsT = rowsT_s[:, :].bitcast(BF16)

        emb_t = combo_s[:, 0:4 * 4 * D_EMB].rearrange("p (k j d) -> p k j d", k=4, j=4)
        eT1 = combo_s[:, 4096:4096 + 2 * 500].rearrange("p (k n) -> p k n", k=2)
        eT2 = combo_s[:, 5120:5120 + 2 * 500].rearrange("p (k n) -> p k n", k=2)
        proj_t = combo_s[:, 6144:6144 + 4 * 256].rearrange("p (k n) -> p k n", k=4)
        src_t = combo_s[:, 8192:8192 + 2048].rearrange("p (g s d) -> p g s d", g=8, s=SPAN)
        mean_t = combo_s[:, 10240:10240 + 512].rearrange("p (g d) -> p g d", g=8)
        meanT = combo_s[:, 10752:10752 + 1024]
        hidT = combo_s[:, 11776:11776 + 2048].rearrange("p (m n) -> p m n", m=2)
        comp_t = combo_s[:, 13824:13824 + 512].rearrange("p (g d) -> p g d", g=8)
        tgt_row = hot_s[:, 0:ROUNDS * N_SPAN].rearrange("p (r n) -> p r n", r=ROUNDS)
        later = hot_s[:, 3072:3072 + 1024]
        same = parts_s[:, 0:1024]
        junk = parts_s[:, 1024:2048]

        id_f = sb("id_f", [P, P], F32)
        id_b = sb("id_b", [P, P], BF16)
        flip = combo_s[:, 14336:14336 + P]
        triT = sb("triT", [P, P], F32)
        toepT = sb("toepT", [P, P], F32)
        toep_raw = combo_s[:, 14464:14464 + P]
        toep_mid = combo_s[:, 14592:14592 + P]
        causal = sb("causal", [P, P], F32)
        sel_s = sb("sel_s", [ROWS, P], BF16)
        sel_d = sb("sel_d", [ROWS, P], BF16)
        key_no = sb("key_no", [P, KEYS, TOPK], BF16)
        rank_w = sb("rank_w", [P, TOPK], BF16)
        half = sb("half", [P, 1], F32)
        fence_t = sb("fence_t", [P, 2], F32)
        wd1 = combo_s[:, 14720:14720 + C]
        wd2 = combo_s[:, 14784:14784 + C]
        wc1_t = combo_s[:, 14848:14848 + 256]
        wc2_t = combo_s[:, 15104:15104 + 128].rearrange("p (m n) -> p m n", m=2)
        ones_r = combo_s[:, 15232:15232 + P]
        bc2_t = combo_s[:, 15360:15360 + C]
        pkq = table_s[:, 0:512]
        keys_t = table_s[:, 512:1024]
        pkqT = table_s[:, 1024:1280].rearrange("p (k c) -> p k c", k=4)
        keysT = table_s[:, 1280:1536].rearrange("p (k c) -> p k c", k=4)
        rowbuf = table_s[:, 0:N_TOK * C // P]
        w_mix = sb("w_mix", [P, 3 * C], F32)
        mixes = sb("mixes", [P, 4], F32)
        wo_a = sb("wo_a", [C, C], F32)
        pk_m = sb("pk_m", [C, 2 * HEADS * KEYS], F32)
        wq_t = sb("wq_t", [C, HEADS * C], F32)
        wo_f = sb("wo_f", [P, HEADS, C], F32)
        ids_i = combo_s[:, 15424:15424 + P].bitcast(I32)
        ids_f = combo_s[:, 15552:15552 + P]
        ids_n = combo_s[:, 15680:15680 + P]
        ids_u = combo_s[:, 15808:15808 + P].bitcast(U32)
        sp_i = combo_s[:, 15936:15936 + 96].bitcast(I32).rearrange("p (r m s) -> p r m s", r=ROUNDS, m=8)
        sp_f = combo_s[:, 16032:16032 + 96].rearrange("p (r m s) -> p r m s", r=ROUNDS, m=8)
        sp_n = combo_s[:, 16128:16128 + 96].rearrange("p (r m s) -> p r m s", r=ROUNDS, m=8)
        sp_u = combo_s[:, 16224:16224 + 96].bitcast(U32).rearrange("p (r m s) -> p r m s", r=ROUNDS, m=8)
        sp_m = sb("sp_m", [P, ROUNDS, 8, SPAN], F32)
        tg_f = sb("tg_f", [P, ROUNDS, 8], F32)
        tg_n = sb("tg_n", [P, ROUNDS, 8], F32)
        tg_u = sb("tg_u", [P, ROUNDS, 8], U32)
        dup = sb("dup", [P, ROUNDS, 8], F32)
        n_in = sb("n_in", [P, ROUNDS, 8], F32)

        E = sb("E", [P, 2, BT], F32)
        W = sb("W", [P, 4, BT], F32)
        kv_out = sb("kv_out", [P, 2, BT], F32)
        h0 = sb("h0", [P, C], F32)
        stats = sb("stats", [P, 6], F32)
        mv = sb("mv", [P, 2], F32)
        rstd = sb("rstd", [P, 1], F32)
        vareps = sb("vareps", [P, 1], F32)
        xn2 = sb("xn2", [P, 2, C], F32)
        xxT = sb("xxT", [P, T], F32)
        k_e = sb("k_e", [P, C], F32)
        k_c = sb("k_c", [P, C], F32)
        kv_t = sb("kv_t", [P, C], F32)
        e_r = sb("e_r", [P, C], F32)
        den = sb("den", [P, C], F32)
        rden = sb("rden", [P, C], F32)
        rwkv = sb("rwkv", [P, C], F32)
        rwT = sb("rwT", [C, T], F32)
        h1 = sb("h1", [P, C], F32)
        xn = sb("xn", [P, C], F32)
        xnT = sb("xnT", [C, T], F32)
        sim = sb("sim", [P, 2, HEADS, KEYS], F32)
        simr = sb("simr", [P, 2, HEADS, KEYS], F32)
        top = sb("top", [P, 2, HEADS, TOPK], F32)
        idx = sb("idx", [P, 2, HEADS, TOPK], U32)
        idx_b = sb("idx_b", [P, 2, HEADS, TOPK], BF16)
        cand = sb("cand", [P, HEADS, PAIRS], F32)
        candr = sb("candr", [P, HEADS, PAIRS], F32)
        picked = cand
        expd = sb("expd", [P, HEADS, PAIRS], F32)
        top_a = sb("top_a", [P, HEADS, 8], F32)
        top_b = sb("top_b", [P, HEADS, 8], F32)
        zsum = sb("zsum", [P, HEADS], F32)
        lnz = sb("lnz", [P, HEADS], F32)
        shift0 = sb("shift0", [P, HEADS], F32)
        count = sb("count", [P, HEADS, TOPK], BF16)
        resid = simr
        kv_c = sb("kv_c", [P, HEADS, T], F32)
        xnT_c = sb("xnT_c", [C, T], F32)
        h1_c = sb("h1_c", [P, C], F32)
        qT = sb("qT", [C, 4, T], F32)
        att = sb("att", [P, 4, T], F32)
        attT = sb("attT", [P, 4, T], F32)
        vo = sb("vo", [P, 4, C], F32)
        nmax = sb("nmax", [P, 4], F32)
        asum = sb("asum", [P, 4], F32)
        rsum = sb("rsum", [P, 4], F32)
        res = sb("res", [P, C], F32)

        PS = [pb("ps_s0"), pb("ps_s1")]
        PD = [pb("ps_d0"), pb("ps_d1")]
        PO = pb("ps_o")
        XA = pb("ps_a")
        XC = pb("ps_c")
        XO = pb("ps_x")
        XAb = XA[:, :].bitcast(BF16)

        names = """loads_w loads_p loads_q loads_x loads_sp emb_in0 emb_in1 emb_in2 emb_in3 emb_tr
        emb_c1 emb_c2 emb_mm emb_out proj_w0 proj_w1 proj_w2 proj_w3 consts ids_ok sp_ok span_ok tw_w tw_in tgt_w
        tgt_in dup_ok tok_in buf_w src_in masked summed mean_ok mean_tr mean_c hid_mm hid_ok comp_mm
        comp_ok scat_ok misc_pe misc_v misc_a pk_tr pk_c pk_step pk_ok mix_ok toep_tr toep_c toep_mm toep_ok
        tab_w combo_in0 combo_in1 scores_ready exp_ready weights_ready pv_done kv_ready kv_w
        h0_in var1_ok rstd1_ok xn2_ok xn2_tr xxT_ok kvr_mm kclip_ok er_ok k_ok kv_ok scan_mm den_ok
        rden_ok rwkv_ok rw_tr rwT_ok proj_mm h1_ok stat1_ok stat2_ok var2_ok rstd2_ok xn_ok xn_tr xnT_ok h1_w xn_w
        sim0_mm sim0_ok sim1_mm sim1_ok topk_step idxb_ok cand_ok gap_ok expd_ok stair_step
        picked_ok weighed_ok z_ok lnz_ok shift_ok count_ok shifted_ok high_ok resid_ok mid_ok low_ok
        hot0_ok hot1_ok weigh0_ok weigh1_ok tree1_step tree0_step rows_tr rows_c rows_w c_in q_mm q_ok
        att_mm vo_mm vo_ok masked_ok nmax_ok aexp_ok rsum_ok att_ok att_tr attT_ok o_mm res_ok out_w
        fence_v ve1_ok ve2_ok""".split()
        S = {n: sem(n) for n in names}
        block = ctx.enter_context(nc.Block())

        sp_src = [s.rearrange("(p g) s -> p g s", g=8) for s in (spans0, spans1, spans2)]
        emb_v = emb_table.rearrange("(t p) d -> p t d", p=125)
        proj_v = proj_d.rearrange("(t p) d -> p t d", p=125)
        keys_v = keys_table.rearrange("(h g j i2 i) d -> h j i g i2 d", h=HEADS, g=NJ, j=CJ, i2=NI)
        vals_v = values_table.rearrange("(h g j i2 i) d -> h j i g i2 d", h=HEADS, g=NJ, j=CJ, i2=NI)

        @block.sync
        def _(sp):
            sp.dma_start(ids_i, x).then_inc(S["loads_x"], 16)
            for r in range(ROUNDS):
                sp.dma_start(sp_i[:, r], sp_src[r]).then_inc(S["loads_sp"], 16)
            sp.dma_start(wd1, w_down[0:P, :]).then_inc(S["loads_w"], 16)
            sp.dma_start(wd2[0:C], w_down[P:D_EMB, :]).then_inc(S["loads_w"], 16)
            sp.dma_start(wd2[C:C + 1], b_down[None, :]).then_inc(S["loads_w"], 16)
            for k in range(4):
                sp.dma_start(emb_t[0:125, k], emb_v[:, 4 * k:4 * k + 4, :]).then_inc(S[f"emb_in{k}"], 16)
            with sp.Fori(1, 4) as i:
                for k in range(4):
                    sp.wait_ge(S["emb_tr"], 4 * i + k - 3)
                    sp.dma_start(emb_t[0:125, k], emb_v[:, bass.ds(16 * i + 4 * k, 4), :]).then_inc(
                        S[f"emb_in{k}"], 16)
            sp.dma_start(wc1_t[0:C], wc1).then_inc(S["loads_p"], 16)
            sp.dma_start(wc1_t[C:C + 1], bc1[None, :]).then_inc(S["loads_p"], 16)
            sp.dma_start(wc2_t, wc2.rearrange("(m k) n -> k m n", m=2)).then_inc(S["loads_p"], 16)
            sp.dma_start(bc2_t[0:1], bc2[None, :]).then_inc(S["loads_p"], 16)
            for lo in (0, C):
                for n, w in enumerate((Wk, Wv, Wr)):
                    sp.dma_start(w_mix[lo:lo + C, n * C:(n + 1) * C], w).then_inc(S["loads_q"], 16)
                for n, m in enumerate((mix_k, mix_v, mix_r)):
                    with nc.allow_non_contiguous_dma(reason="64 channel weights, once"):
                        sp.dma_start(mixes[lo:lo + C, n:n + 1], m.rearrange("a b c -> (a b) c").rearrange(
                            "a c -> c a")).then_inc(S["loads_q"], 16)
            sp.dma_start(wo_a[:, :], Wo).then_inc(S["loads_q"], 16)
            sp.dma_start(wq_t[:, :], Wq).then_inc(S["loads_q"], 16)
            sp.dma_start(wo_f[C:P], Wo_ffn.rearrange("(h d) n -> d h n", h=HEADS)).then_inc(S["loads_q"], 16)
            sp.dma_start(pkq[0:C], Wq_pk).then_inc(S["loads_q"], 16)
            for p_ in range(2):
                sp.dma_start(keys_t[0:C, p_ * 256:(p_ + 1) * 256],
                             pk_keys[p_].rearrange("k h d -> k (h d)")).then_inc(S["loads_q"], 16)
            sp.dma_start(tw_d[0:1, :], time_w[None, TIME_LEN - T:]).then_inc(S["tw_w"], 16)
            sp.wait_ge(S["consts"], 16)
            sp.dma_start(tw_d[1:2, :], junk[0:1, 0:T]).then_inc(S["tw_w"], 16)
            sp.wait_ge(S["tw_w"], 32)
            tw_rows = bass.AP(tensor=tw_d.tensor, offset=0, ap=[[1, P], [1, P]])
            sp.dma_start(toep_raw, tw_rows).then_inc(S["tw_in"], 16)
            sp.wait_ge(S["sp_ok"], 1)
            for r in range(ROUNDS):
                sp.dma_start(tgt_d[r].rearrange("(p g) -> p g", g=8), tg_f[:, r]).then_inc(S["tgt_w"], 16)
            sp.wait_ge(S["tgt_w"], 16 * ROUNDS)
            for r in range(ROUNDS):
                sp.dma_start(tgt_row[:, r], tgt_d[r:r + 1, :].to_broadcast([P, N_SPAN])).then_inc(
                    S["tgt_in"], 16)
            with sp.Fori(0, HEADS) as h:
                for kv, tab in enumerate((keys_v, vals_v)):
                    for j in range(CJ):
                        for i2 in range(NI):
                            sp.dma_start(
                                tab_d[h, j * CI:(j + 1) * CI].rearrange(
                                    "i (g i2) d -> i g i2 d", i2=NI)[:, :, i2, kv * C:(kv + 1) * C],
                                tab[h, j, :, :, i2, :]).then_inc(S["tab_w"], 16)
            sp.wait_ge(S["tok_in"], 16 * P)
            sp.dma_start(buf_d.rearrange("(p j) d -> p (j d)", p=P), rowbuf).then_inc(S["buf_w"], 16)

            def snap(value):
                return value if isinstance(value, int) else sp.snap(value)

            def load_unit(u, head, k, done, rows):
                wait(sp, S["pv_done"], done)
                sp.wait_ge(S["rows_w"], rows)
                for g in range(NI):
                    src = rows_d[u, g * SIDE0_ROWS:(g + 1) * SIDE0_ROWS, :]
                    dst = combo[0:SIDE0_ROWS, k].rearrange("p (gj gi) t -> p gj gi t", gi=NI)[:, :, g, :]
                    sp.dma_start(dst, src[:, None, :].to_broadcast([SIDE0_ROWS, NJ, BT])).then_inc(
                        S[f"combo_in{k}"], 16)
                for g in range(NJ):
                    src = rows_d[u, SIDE_ROWS + g * SIDE1_ROWS:SIDE_ROWS + (g + 1) * SIDE1_ROWS, :]
                    sp.dma_start(combo[SIDE0_ROWS:ROWS, k, g * NI:(g + 1) * NI, :],
                                 src[:, None, :].to_broadcast([SIDE1_ROWS, NI, BT])).then_inc(
                        S[f"combo_in{k}"], 16)
                sp.dma_start(table[:, k], tab_d[head]).then_inc(S[f"combo_in{k}"], 16)

            def window(t, F, Tl, Bb, Cc, first=False, last=False):
                b, w, c = t + 1, t - 4, t - 8
                done1, done2 = SLOTS * w, SLOTS * w + CHUNKS
                rows1, rows2 = 16 * w + 16, 16 * t + 16 if Tl else 16 * B
                tb, tq = snap(t // BLOCK), snap(t % BLOCK)
                head1, head2 = snap((2 * t + 1) % HEADS), snap((2 * t + 2) % HEADS)
                if F:
                    wait(sp, S["h1_ok"], b)
                    wait(sp, S["buf_w"], 16)
                    sp.wait_ge(S["scat_ok"], ROUNDS * 8 * 16)
                    sp.dma_start(h0[:, :], buf_d[bass.ds(b * T, T), :]).then_inc(S["h0_in"], 16)
                if Cc:
                    wait(sp, S["res_ok"], 2 * c)
                    sp.wait_ge(S["kv_w"], 16 * 2 * w if Bb else 16 * UNITS)
                    sp.dma_start(kv_c[:, :, :], kv_d[bass.ds((tb - 2) * HEADS, HEADS), :, bass.ds(tq * T, T)].rearrange(
                        "h p t -> p h t")).then_inc(S["c_in"], 16)
                    sp.wait_ge(S["h1_w"], 16 * (c + 1))
                    sp.wait_ge(S["xn_w"], 16 * (c + 1))
                    sp.dma_start(h1_c[:, :], h1_d[bass.ds(c, 1)].rearrange("a t c -> (a t) c")).then_inc(S["c_in"], 16)
                    sp.dma_start(xnT_c[:, :], xn_d[bass.ds(c, 1)].rearrange("a c t -> (a c) t")).then_inc(S["c_in"], 16)
                if Bb:
                    load_unit(2 * w + 1, head1, 1, done1, rows1)
                if F:
                    sp.wait_ge(S["h1_ok"], b + 1)
                    sp.dma_start(h1_d[bass.ds(b, 1)].rearrange("a t c -> (a t) c"), h1[:, :]).then_inc(S["h1_w"], 16)
                    sp.wait_ge(S["xnT_ok"], b + 1)
                    sp.dma_start(xn_d[bass.ds(b, 1)].rearrange("a c t -> (a c) t"), xnT[:, :]).then_inc(S["xn_w"], 16)
                if Bb:
                    sp.wait_ge(S["kv_ready"], 2 * w + 1)
                    sp.dma_start(kv_d[bass.ds(2 * w, 1)].rearrange("a p t -> (a p) t"), kv_out[:, 0, :]).then_inc(
                        S["kv_w"], 16)
                if Tl:
                    sp.wait_ge(S["rows_c"], 4 * (t + 1))
                    dst = rows_d[bass.ds(tb * HEADS, HEADS), :, bass.ds(tq * T, T)].rearrange(
                        "h (k p) t -> p (h k) t", p=P)
                    sp.dma_start(dst, rowsT.rearrange("p (k t) -> p k t", t=T)).then_inc(S["rows_w"], 16)
                if (Bb and not last) or first:
                    if first:
                        sp.wait_ge(S["tab_w"], 16 * HEADS * 2 * CJ * NI)
                        sp.wait_ge(S["pk_ok"], 2)
                    load_unit(2 * w + 2, head2, 0, done2 if Bb else 0, rows2)
                if Cc:
                    sp.wait_ge(S["res_ok"], 2 * c + 2)
                    sp.dma_start(out[bass.ds(c, 1)].rearrange("a t c -> (a t) c"), res[:, :]).then_inc(S["out_w"], 16)
                if Bb:
                    sp.wait_ge(S["kv_ready"], 2 * w + 2)
                    sp.dma_start(kv_d[bass.ds(2 * w + 1, 1)].rearrange("a p t -> (a p) t"), kv_out[:, 1, :]).then_inc(
                        S["kv_w"], 16)

            run_windows(sp, window)
            sp.wait_ge(S["out_w"], 16 * B)
            sp.wait_ge(S["kv_w"], 16 * UNITS)
            sp.wait_ge(S["rows_w"], 16 * B)
            sp.wait_ge(S["h1_w"], 16 * B)
            sp.wait_ge(S["xn_w"], 16 * B)

        @block.gpsimd
        def _(pool):
            g = nc.gpsimd
            cs = S["consts"]
            g.memset(id_f[:, :], 0.0).then_inc(cs, 1)
            g.memset(id_b[:, :], 0.0).then_inc(cs, 1)
            g.memset(flip, 0.0).then_inc(cs, 1)
            g.memset(triT[:, :], 1.0).then_inc(cs, 1)
            g.memset(causal[:, :], 0.0).then_inc(cs, 1)
            g.memset(sel_s[:, :], 0.0).then_inc(cs, 1)
            g.memset(sel_d[:, :], 0.0).then_inc(cs, 1)
            g.memset(half[:, :], -0.5).then_inc(cs, 1)
            g.memset(junk[:, 0:T], 0.0).then_inc(cs, 1)
            g.memset(ones_r, 1.0).then_inc(cs, 1)
            g.memset(xxT[:, :], 0.0).then_inc(cs, 1)
            for n, m in enumerate((eT2[C:C + 1], meanT[C:C + 1])):
                pool.wait_ge(cs, 11 + n)
                g.memset(m, 1.0).then_inc(cs, 1)
            pool.wait_ge(cs, 13)
            g.iota(key_no[:, :, :], [[1, KEYS], [0, TOPK]], base=0, channel_multiplier=0,
                   allow_small_or_imprecise_dtypes=True).then_inc(cs, 1)
            g.iota(rank_w[:, :], [[-1, TOPK]], base=TOPK, channel_multiplier=0,
                   allow_small_or_imprecise_dtypes=True).then_inc(cs, 1)
            g.iota(later, [[1, N_SPAN]], base=0, channel_multiplier=-8,
                   allow_small_or_imprecise_dtypes=True).then_inc(cs, 1)
            pool.wait_ge(cs, 16)
            for m, base, step, op, fill in ((id_f[:, :], 0, -1, ALU.not_equal, 1.0),
                                            (id_b[:, :], 0, -1, ALU.not_equal, 1.0),
                                            (flip, -(P - 1), 1, ALU.not_equal, 1.0)):
                g.affine_select(out=m, in_=m, pattern=[[step, P]], compare_op=op, fill=fill, base=base,
                                channel_multiplier=1).then_inc(cs, 1)
            g.affine_select(out=triT[:, :], in_=triT[:, :], pattern=[[1, P]], compare_op=ALU.is_ge,
                            fill=0.0, base=0, channel_multiplier=-1).then_inc(cs, 1)
            g.affine_select(out=causal[:, :], in_=causal[:, :], pattern=[[-1, P]], compare_op=ALU.is_ge,
                            fill=MASKED, base=0, channel_multiplier=1).then_inc(cs, 1)
            n = 21
            for m, s0, s1 in ((sel_s, (0, CI, 2 * CI), (SIDE0_ROWS, SIDE0_ROWS + CJ, SIDE0_ROWS + 2 * CJ)),
                              (sel_d, (3 * CI,), (SIDE0_ROWS + 3 * CJ,))):
                v = m[:, :].rearrange("r (j i) -> r j i", i=CI)
                for base, pat in [(s, [[0, CJ], [-1, CI]]) for s in s0] + [(s, [[-1, CJ], [0, CI]]) for s in s1]:
                    pool.wait_ge(cs, n)
                    g.affine_select(out=v, in_=v, pattern=pat, compare_op=ALU.not_equal, fill=1.0,
                                    base=-base, channel_multiplier=1).then_inc(cs, 1)
                    n += 1
            pool.wait_ge(S["ids_ok"], 1)
            for k in range(4):
                pool.wait_ge(S[f"proj_w{k}"], 64)
            pool.wait_ge(S["pk_step"], 2 * HEADS)
            for j in range(P):
                g.indirect_dma_start(rowbuf[:, j * C:(j + 1) * C], None, proj_d,
                                     bass.IndirectOffsetOnAxis(ids_u[:, j:j + 1], 0)).then_inc(S["tok_in"], 16)
            pool.wait_ge(S["buf_w"], 16)
            pool.wait_ge(S["span_ok"], 1)
            for r in range(ROUNDS):
                if r:
                    pool.wait_ge(S["scat_ok"], 128 * r)
                    pool.wait_ge(S["masked"], r)
                for m in range(8):
                    for s in range(SPAN):
                        g.indirect_dma_start(src_t[:, m, s, :], None, buf_d,
                                             bass.IndirectOffsetOnAxis(sp_u[:, r, m, s:s + 1], 0)).then_inc(
                            S["src_in"], 16)
                pool.wait_ge(S["dup_ok"], 1)
                pool.wait_ge(S["comp_ok"], r + 1)
                pool.wait_ge(S["src_in"], 16 * 32 * (r + 1))
                for m in range(8):
                    g.indirect_dma_start(buf_d, bass.IndirectOffsetOnAxis(tg_u[:, r, m:m + 1], 0),
                                         comp_t[:, m, :], None, bounds_check=N_TOK - 1,
                                         oob_is_err=False).then_inc(S["scat_ok"], 16)

            def front(s, b):
                if s == 4:
                    pool.wait_ge(S["ve1_ok"], b + 1)
                    g.tensor_tensor(rstd[:, :], vareps[:, :], half[:, :], ALU.pow).then_inc(S["rstd1_ok"], 1)
                if s == 24:
                    pool.wait_ge(S["ve2_ok"], b + 1)
                    g.tensor_tensor(rstd[:, :], vareps[:, :], half[:, :], ALU.pow).then_inc(S["rstd2_ok"], 1)

            def tail(s, t):
                if s == 0:
                    pool.wait_ge(S["shift_ok"], t + 1)
                    wait(pool, S["low_ok"], 2 * t)
                    g.tensor_tensor(resid[:, 0], sim[:, 0], shift0[:, :, None].to_broadcast([P, HEADS, KEYS]),
                                    ALU.subtract).then_inc(S["shifted_ok"], 1)
                    g.tensor_tensor(resid[:, 1], sim[:, 1], top[:, 1, :, 0:1].to_broadcast([P, HEADS, KEYS]),
                                    ALU.subtract).then_inc(S["shifted_ok"], 1)
                if s in (5, 10):
                    if s == 5:
                        pool.wait_ge(S["high_ok"], 2 * (t + 1))
                    else:
                        pool.wait_ge(S["mid_ok"], 2 * (t + 1))
                    for side, pt in enumerate((parts0, parts1)):
                        v = resid[:, side].rearrange("p h (g i) -> p h g i", i=(CI, CJ)[side])
                        if s == 5:
                            g.tensor_tensor(v, v, pt[:, :, :, 0, :], ALU.subtract).then_inc(S["resid_ok"], 1)
                        else:
                            g.tensor_tensor(pt[:, :, :, 2, :], v, pt[:, :, :, 1, :], ALU.subtract).then_inc(
                                S["low_ok"], 1)
                if 6 <= s < 6 + HEADS:
                    h = s - 6
                    if h % 2 == 0:
                        pool.wait_ge(S["hot0_ok"], 4 * t + h // 2 + 1)
                    if h == 0:
                        pool.wait_ge(S["count_ok"], t + 1)
                    g.tensor_tensor(hot[:, 0, h], hot[:, 0, h],
                                    count[:, h, None, :].to_broadcast([P, KEYS, TOPK]), ALU.mult).then_inc(
                        S["weigh0_ok"], 1)

            def window(t, F, Tl, Bb, Cc, first=False, last=False):
                for s in range(SLOTS):
                    if Tl:
                        tail(s, t)
                    if F:
                        front(s, t + 1)
            run_windows(pool, window)

        @block.tensor
        def _(pe):
            mm, tr = nc.tensor.matmul, nc.tensor.transpose

            def fence(column):
                mm(column, id_b[:, :], id_b[:, 0:1], start=True, stop=True)

            pe.wait_ge(S["consts"], 29)
            pe.wait_ge(S["loads_w"], 48)
            with pe.Fori(0, 4) as i:
                for k in range(4):
                    n = 4 * i + k
                    e = k % 2
                    pe.wait_ge(S[f"emb_in{k}"], 16 * (i + 1))
                    pe.wait_ge(S["emb_c1"], n - 1 if k > 1 else n) if k > 0 else None
                    pe.wait_ge(S["emb_c2"], n - 1 if k > 1 else n) if k > 0 else None
                    if k == 0:
                        pe.wait_ge(S["emb_c1"], n)
                        pe.wait_ge(S["emb_c2"], n)
                    for j in range(4):
                        tr(PS[e][:, j * 125:(j + 1) * 125], emb_t[0:125, k, j, 0:P], id_f[0:125, 0:125])
                        last = tr(PD[e][0:C, j * 125:(j + 1) * 125], emb_t[0:125, k, j, P:D_EMB], id_f[0:125, 0:125])
                    last.then_inc(S["emb_tr"], 1)
                    pe.wait_ge(S["emb_c1"], n + 1)
                    pe.wait_ge(S["emb_c2"], n + 1)
                    o = (XA, XC)[e]
                    if k > 1:
                        pe.wait_ge(S["emb_out"], n - 1)
                    else:
                        pe.wait_ge(S["emb_out"], n)
                    for j in range(4):
                        mm(o[0:125, j * C:(j + 1) * C], eT1[:, e, j * 125:(j + 1) * 125], wd1, start=True, stop=False)
                        last = mm(o[0:125, j * C:(j + 1) * C], eT2[0:C + 1, e, j * 125:(j + 1) * 125],
                                  wd2[0:C + 1], start=False, stop=True)
                    last.then_inc(S["emb_mm"], 1)
            pe.wait_ge(S["loads_q"], 18 * 16)
            pe.wait_ge(S["emb_out"], 16)
            for k in range(4):
                tr(PS[0][:, k * C:(k + 1) * C], pkq[0:C, k * P:(k + 1) * P], id_f[0:C, 0:C])
                last = tr(PS[1][:, k * C:(k + 1) * C], keys_t[0:C, k * P:(k + 1) * P], id_f[0:C, 0:C])
            last.then_inc(S["pk_tr"], 1)
            pe.wait_ge(S["pk_c"], 2)
            for n in range(2 * HEADS):
                wait(pe, S["pk_step"], n)
                k, r = n // 4, (n % 4) * D_KEY
                last = mm(PD[n // HEADS][0:C, (n % HEADS) * KEYS:(n % HEADS + 1) * KEYS],
                          pkqT[r:r + D_KEY, k, :], keysT[r:r + D_KEY, k, :], start=True, stop=True)
                last.then_inc(S["pk_step"], 1)
            pe.wait_ge(S["tw_in"], 16)
            tr(PO[:, 0:P], toep_raw, id_f[:, :]).then_inc(S["toep_tr"], 1)
            pe.wait_ge(S["toep_c"], 1)
            mm(PO[:, P:2 * P], toep_mid, flip, start=True, stop=True).then_inc(S["toep_mm"], 1)
            pe.wait_ge(S["loads_p"], 64)
            pe.wait_ge(S["pk_ok"], 2)
            pe.wait_ge(S["toep_ok"], 1)
            for r in range(ROUNDS):
                pe.wait_ge(S["mean_ok"], r + 1)
                for m in range(8):
                    last = tr((XA, XC)[m // 4][0:C, (m % 4) * P:(m % 4 + 1) * P], mean_t[:, m, :], id_f[:, :])
                last.then_inc(S["mean_tr"], 1)
                pe.wait_ge(S["mean_c"], 2 * (r + 1))
                for m in range(2):
                    for n in range(2):
                        last = mm((PS, PD)[m][n][:, :], wc1_t[0:C + 1, m * P:(m + 1) * P],
                                  meanT[0:C + 1, n * 512:(n + 1) * 512], start=True, stop=True)
                        last.then_inc(S["hid_mm"], 1)
                pe.wait_ge(S["hid_ok"], 4 * (r + 1))
                for m in range(8):
                    o = XO[:, m * C:(m + 1) * C]
                    for k in range(2):
                        mm(o, hidT[:, k, m * P:(m + 1) * P], wc2_t[:, k, :], start=k == 0, stop=False)
                    last = mm(o, ones_r[0:1, :], bc2_t[0:1, :], start=False, stop=True)
                last.then_inc(S["comp_mm"], 1)
            pe.wait_ge(S["comp_ok"], ROUNDS)

            def chunk_scores(s, w):
                k, c, e = s // CHUNKS, s % CHUNKS, s % 2
                if c == 0:
                    pe.wait_ge(S[f"combo_in{k}"], LOAD_UNIT * (w + 1))
                if s >= 2:
                    pe.wait_ge(S["weights_ready"], SLOTS * w + s - 1)
                else:
                    wait(pe, S["weights_ready"], SLOTS * w)
                mm(PS[e][:, :], sel_s[:, :], combo[0:ROWS, k, c, :], start=True, stop=True)
                mm(PD[e][:, :], sel_d[:, :], combo[0:ROWS, k, c, :], start=True, stop=True).then_inc(
                    S["scores_ready"], 1)

            def chunk_sum(s, w):
                k, c = s // CHUNKS, s % CHUNKS
                if c == 0:
                    wait(pe, S["kv_ready"], 2 * w + k)
                pe.wait_ge(S["weights_ready"], SLOTS * w + s + 1)
                mm(PO[:, :], table[:, k, c, :], W[:, s % 4, :], start=c == 0, stop=c == CHUNKS - 1).then_inc(
                    S["pv_done"], 1)

            def front(s, b):
                if s == 7:
                    pe.wait_ge(S["xn2_ok"], b + 1)
                    wait(pe, S["sim1_ok"], b)
                    wait(pe, S["rows_c"], 4 * (b - 1)) if isinstance(b, int) else pe.wait_ge(S["rows_c"], 4 * b - 4)
                    fence(XA[:, 0:1])
                    tr(XA[:, 0:P], xn2[:, :, :].rearrange("p a c -> p (a c)"), id_f[:, :]).then_inc(S["xn2_tr"], 1)
                if s == 10:
                    pe.wait_ge(S["xxT_ok"], 2 * (b + 1))
                    mm(XA[:, 0:3 * C], xxT[:, :], w_mix[:, :], start=True, stop=True).then_inc(S["kvr_mm"], 1)
                if s == 14:
                    pe.wait_ge(S["k_ok"], b + 1)
                    pe.wait_ge(S["kv_ok"], b + 1)
                    mm(XA[:, 192:256], triT[:, :], k_e[:, :], start=True, stop=True)
                    mm(XA[:, 256:320], toepT[:, :], kv_t[:, :], start=True, stop=True).then_inc(S["scan_mm"], 1)
                if s == 18:
                    pe.wait_ge(S["rwkv_ok"], b + 1)
                    fence(XA[:, 320:321])
                    tr(XA[0:C, 320:448], rwkv[:, :], id_f[:, :]).then_inc(S["rw_tr"], 1)
                if s == 20:
                    pe.wait_ge(S["rwT_ok"], b + 1)
                    fence(XA[:, 448:449])
                    mm(XA[:, 448:512], rwT[:, :], wo_a[:, :], start=True, stop=True).then_inc(S["proj_mm"], 1)
                if s == 26:
                    pe.wait_ge(S["xn_ok"], b + 1)
                    fence(XA[:, 0:1])
                    tr(XA[0:C, 0:P], xn[:, :], id_f[:, :]).then_inc(S["xn_tr"], 1)
                if s == 28:
                    pe.wait_ge(S["xnT_ok"], b + 1)
                    fence(XA[:, 0:1])
                    mm(XA[:, :], xnT[:, :], pk_m[:, 0:512], start=True, stop=True).then_inc(S["sim0_mm"], 1)
                if s == 30:
                    pe.wait_ge(S["sim0_ok"], b + 1)
                    fence(XA[:, 0:1])
                    mm(XA[:, :], xnT[:, :], pk_m[:, 512:1024], start=True, stop=True).then_inc(S["sim1_mm"], 1)

            def tail(s, t, F):
                if s in (32, 34, 36, 38):
                    n = (s - 32) // 2
                    if n == 0:
                        pe.wait_ge(S["tree0_step"], 5 * (t + 1))
                        pe.wait_ge(S["tree1_step"], 5 * (t + 1))
                        pe.wait_ge(S["low_ok"], 2 * (t + 1))
                        if F:
                            pe.wait_ge(S["sim1_ok"], t + 2)
                    else:
                        pe.wait_ge(S["rows_c"], 4 * t + n)
                    fence(XA[:, 0:1])
                    for j in range(8):
                        m = 8 * n + j
                        last = tr(XAb[:, j * P:(j + 1) * P], parts[:, m * P:(m + 1) * P], id_b[:, :])
                    last.then_inc(S["rows_tr"], 1)

            def attend(s, c):
                for hg, base in ((0, 38), (1, 50)):
                    n = 2 * c + hg
                    if s == base:
                        if hg == 0:
                            pe.wait_ge(S["c_in"], 48 * (c + 1))
                        wait(pe, S["attT_ok"], n)
                        fence(XC[:, 0:1])
                        for h in range(4):
                            last = mm(XC[0:C, h * T:(h + 1) * T], wq_t[:, (4 * hg + h) * C:(4 * hg + h + 1) * C],
                                      xnT_c[:, :], start=True, stop=True)
                        last.then_inc(S["q_mm"], 1)
                    if s == base + 2:
                        pe.wait_ge(S["q_ok"], n + 1)
                        wait(pe, S["vo_ok"], n)
                        wait(pe, S["res_ok"], n)
                        fence(XC[:, 0:1])
                        for h in range(4):
                            last = mm(XC[:, h * T:(h + 1) * T], qT[:, h, :], kv_c[0:C, 4 * hg + h, :],
                                      start=True, stop=True)
                        last.then_inc(S["att_mm"], 1)
                        for h in range(4):
                            last = mm(XO[:, h * C:(h + 1) * C], kv_c[C:P, 4 * hg + h, :], wo_f[C:P, 4 * hg + h, :],
                                      start=True, stop=True)
                        last.then_inc(S["vo_mm"], 1)
                    if s == base + 9:
                        pe.wait_ge(S["att_ok"], n + 1)
                        fence(XC[:, 0:1])
                        for h in range(4):
                            last = tr(XC[:, h * T:(h + 1) * T], att[:, h, :], id_f[:, :])
                        last.then_inc(S["att_tr"], 1)
                    if s == base + 11:
                        pe.wait_ge(S["attT_ok"], n + 1)
                        pe.wait_ge(S["vo_ok"], n + 1)
                        fence(XO[:, 0:1])
                        for h in range(4):
                            last = mm(XO[:, 256:256 + C], attT[:, h, :], vo[:, h, :],
                                      start=h == 0, stop=h == 3)
                        last.then_inc(S["o_mm"], 1)

            def window(t, F, Tl, Bb, Cc, first=False, last=False):
                w = t - 4
                for s in range(SLOTS):
                    if Bb:
                        chunk_scores(s, w)
                    if F:
                        front(s, t + 1)
                    if Tl:
                        tail(s, t, F)
                    if Cc:
                        attend(s, t - 8)
                    if Bb and s >= 2:
                        chunk_sum(s - 2, w)
                if Bb:
                    chunk_sum(SLOTS - 2, w)
                    chunk_sum(SLOTS - 1, w)
            run_windows(pe, window)

        @block.scalar
        def _(act):
            a = nc.scalar.activation
            with act.Fori(0, 4) as i:
                for k in range(4):
                    n, e = 4 * i + k, k % 2
                    act.wait_ge(S["emb_tr"], n + 1)
                    if k > 1:
                        act.wait_ge(S["emb_mm"], n - 1)
                    else:
                        act.wait_ge(S["emb_mm"], n)
                    a(eT1[:, e, :], PS[e][:, 0:500], ACT.Copy).then_inc(S["emb_c1"], 1)
                    act.wait_ge(S["emb_mm"], n + 1)
                    act.wait_ge(S[f"proj_w{k}"], 16 * i)
                    a(proj_t[0:125, k, :], (XA, XC)[e][0:125, 0:256], ACT.Copy).then_inc(S["emb_out"], 1)
                    act.wait_ge(S["emb_out"], n + 1)
                    act.dma_start(proj_v[:, bass.ds(4 * n, 4), :],
                                  proj_t[0:125, k, :].rearrange("p (j d) -> p j d", j=4)).then_inc(
                        S[f"proj_w{k}"], 16)
            act.wait_ge(S["pk_tr"], 1)
            a(pkqT, PS[0][:, 0:256].rearrange("p (k c) -> p k c", k=4), ACT.Copy).then_inc(S["pk_c"], 1)
            a(keysT, PS[1][:, 0:256].rearrange("p (k c) -> p k c", k=4), ACT.Copy).then_inc(S["pk_c"], 1)
            for n in range(2):
                act.wait_ge(S["pk_step"], HEADS * (n + 1))
                a(pk_m[:, n * 512:(n + 1) * 512], PD[n][0:C, :], ACT.Copy).then_inc(S["pk_ok"], 1)
            act.wait_ge(S["toep_tr"], 1)
            a(toep_mid, PO[:, 0:P], ACT.Copy).then_inc(S["toep_c"], 1)
            act.wait_ge(S["toep_mm"], 1)
            a(toepT[:, :], PO[:, P:2 * P], ACT.Copy).then_inc(S["toep_ok"], 1)
            for r in range(ROUNDS):
                act.wait_ge(S["mean_tr"], r + 1)
                a(meanT[0:C, 512:1024], XC[0:C, :], ACT.Copy).then_inc(S["mean_c"], 1)
                for m in range(2):
                    for n in range(2):
                        act.wait_ge(S["hid_mm"], 4 * r + 2 * m + n + 1)
                        a(hidT[:, m, n * 512:(n + 1) * 512], (PS, PD)[m][n][:, :], ACT.Gelu_apprx_tanh).then_inc(
                            S["hid_ok"], 1)

            def chunk_exp(s, w):
                act.wait_ge(S["scores_ready"], SLOTS * w + s + 1)
                a(E[:, s % 2, :], PS[s % 2][:, :], ACT.Exp).then_inc(S["exp_ready"], 1)

            def unit_out(k, w):
                act.wait_ge(S["pv_done"], SLOTS * w + CHUNKS * (k + 1))
                wait(act, S["kv_w"], 2 * 16 * w)
                a(kv_out[:, k, :], PO[:, :], ACT.Copy).then_inc(S["kv_ready"], 1)

            def front(s, b):
                if s == 8:
                    act.wait_ge(S["xn2_tr"], b + 1)
                    a(xxT[0:C, :], XA[0:C, 0:P], ACT.Copy).then_inc(S["xxT_ok"], 1)
                    a(xxT[C:P, 1:T], XA[C:P, 0:T - 1], ACT.Copy).then_inc(S["xxT_ok"], 1)
                if s == 12:
                    act.wait_ge(S["kclip_ok"], b + 1)
                    a(e_r[:, :], XA[:, 128:192], ACT.Exp, scale=-1.0).then_inc(S["er_ok"], 1)
                    a(k_e[:, :], k_c[:, :], ACT.Exp).then_inc(S["k_ok"], 1)
                if s == 19:
                    act.wait_ge(S["rw_tr"], b + 1)
                    a(rwT[:, :], XA[0:C, 320:448], ACT.Copy).then_inc(S["rwT_ok"], 1)
                if s == 27:
                    act.wait_ge(S["xn_tr"], b + 1)
                    wait(act, S["xn_w"], 16 * b)
                    a(xnT[:, :], XA[0:C, 0:P], ACT.Copy).then_inc(S["xnT_ok"], 1)
                for side, at in ((0, 29), (1, 31)):
                    if s == at:
                        act.wait_ge(S[f"sim{side}_mm"], b + 1)
                        wait(act, S["shifted_ok"], 2 * b)
                        a(sim[:, side], XA[:, :].rearrange("p (h k) -> p h k", h=HEADS), ACT.Copy).then_inc(
                            S[f"sim{side}_ok"], 1)
                if s == 52:
                    act.wait_ge(S["gap_ok"], b + 1)
                    a(expd[:, :, :], expd[:, :, :], ACT.Exp).then_inc(S["expd_ok"], 1)
                if s == 61:
                    act.wait_ge(S["z_ok"], b + 1)
                    a(lnz[:, :], zsum[:, :], ACT.Ln).then_inc(S["lnz_ok"], 1)

            def tail(s, t):
                if s in (3, 7):
                    if s == 3:
                        act.wait_ge(S["shifted_ok"], 2 * (t + 1))
                        wait(act, S["rows_tr"], 4 * t)
                    else:
                        act.wait_ge(S["resid_ok"], 2 * (t + 1))
                    part = (s - 3) // 4
                    for side, pt in enumerate((parts0, parts1)):
                        a(pt[:, :, :, part, :], resid[:, side].rearrange("p h (g i) -> p h g i", i=(CI, CJ)[side]),
                          ACT.Copy).then_inc(S[("high_ok", "mid_ok")[part]], 1)
                if s in (33, 35, 37, 39):
                    n = (s - 33) // 2
                    act.wait_ge(S["rows_tr"], 4 * t + n + 1)
                    if n == 0:
                        wait(act, S["rows_w"], 16 * t)
                    a(rowsT[:, n * 1024:(n + 1) * 1024], XAb[:, :], ACT.Copy).then_inc(S["rows_c"], 1)

            def attend(s, c):
                for hg, base in ((0, 38), (1, 50)):
                    n = 2 * c + hg
                    if s == base + 1:
                        act.wait_ge(S["q_mm"], n + 1)
                        a(qT[:, :, :], XC[0:C, :].rearrange("p (h t) -> p h t", h=4), ACT.Copy).then_inc(S["q_ok"], 1)
                    if s == base + 3:
                        act.wait_ge(S["vo_mm"], n + 1)
                        wait(act, S["o_mm"], n)
                        a(vo[:, :, :], XO[:, 0:256].rearrange("p (h d) -> p h d", h=4), ACT.Copy).then_inc(S["vo_ok"], 1)
                    if s == base + 5:
                        act.wait_ge(S["nmax_ok"], n + 1)
                        for h in range(4):
                            a(att[:, h, :], att[:, h, :], ACT.Exp, bias=nmax[:, h:h + 1],
                              accum_out=asum[:, h:h + 1]).then_inc(S["aexp_ok"], 1)
                    if s == base + 10:
                        act.wait_ge(S["att_tr"], n + 1)
                        a(attT[:, :, :], XC[:, :].rearrange("p (h t) -> p h t", h=4), ACT.Copy).then_inc(
                            S["attT_ok"], 1)

            def window(t, F, Tl, Bb, Cc, first=False, last=False):
                w = t - 4
                for s in range(SLOTS):
                    if Bb:
                        chunk_exp(s, w)
                    if Bb and s == CHUNKS + 1:
                        unit_out(0, w)
                    if F:
                        front(s, t + 1)
                    if Tl:
                        tail(s, t)
                    if Cc:
                        attend(s, t - 8)
                if Bb:
                    unit_out(1, w)
            run_windows(act, window)

        @block.vector
        def _(dve):
            v = nc.vector
            v.memset(fence_t[:, :], 0.0).then_inc(S["fence_v"], 1)
            dve.wait_ge(S["fence_v"], 1)

            def fence():
                v.tensor_copy(fence_t[:, 0:1], fence_t[:, 1:2])

            mv_n = [0]

            def step(ins):
                mv_n[0] += 1
                ins.then_inc(S["misc_v"], 1)
                dve.wait_ge(S["misc_v"], mv_n[0])

            def clean(f, n, size, top_ok):
                step(v.tensor_scalar(n, f, 0.0, float(size), ALU.is_lt, ALU.mult))
                step(v.tensor_tensor(f, f, n, ALU.add))

            dve.wait_ge(S["loads_x"], 16)
            step(v.tensor_copy(ids_f, ids_i))
            step(v.tensor_scalar(ids_n, ids_f, PAD, -PAD, ALU.is_equal, ALU.mult))
            step(v.tensor_tensor(ids_f, ids_f, ids_n, ALU.add))
            clean(ids_f, ids_n, VOCAB, True)
            step(v.tensor_scalar(ids_f, ids_f, 0.0, VOCAB - 1.0, ALU.max, ALU.min))
            v.tensor_copy(ids_u, ids_f).then_inc(S["ids_ok"], 1)
            dve.wait_ge(S["loads_sp"], 48)
            step(v.tensor_copy(sp_f[:, :, :, :], sp_i[:, :, :, :]))
            step(v.tensor_reduce(tg_f[:, :, :], sp_f[:, :, :, :], AX.X, ALU.max))
            step(v.tensor_scalar(tg_f[:, :, :], tg_f[:, :, :], 1.0, None, ALU.add))
            clean(tg_f[:, :, :], tg_n[:, :, :], N_TOK, False)
            step(v.tensor_scalar(tg_n[:, :, :], tg_f[:, :, :], 0.0, 1.0e6, ALU.is_lt, ALU.mult))
            v.tensor_tensor(tg_f[:, :, :], tg_f[:, :, :], tg_n[:, :, :], ALU.add).then_inc(S["sp_ok"], 1)
            step(v.tensor_scalar(sp_m[:, :, :, :], sp_f[:, :, :, :], PAD, None, ALU.not_equal))
            step(v.tensor_reduce(n_in[:, :, :], sp_m[:, :, :, :], AX.X, ALU.add))
            step(v.tensor_scalar(n_in[:, :, :], n_in[:, :, :], 1.0, None, ALU.max))
            step(v.reciprocal(n_in[:, :, :], n_in[:, :, :]))
            step(v.tensor_tensor(sp_f[:, :, :, :], sp_f[:, :, :, :], sp_m[:, :, :, :], ALU.mult))
            clean(sp_f[:, :, :, :], sp_n[:, :, :, :], N_TOK, True)
            step(v.tensor_scalar(sp_f[:, :, :, :], sp_f[:, :, :, :], 0.0, N_TOK - 1.0, ALU.max, ALU.min))
            v.tensor_copy(sp_u[:, :, :, :], sp_f[:, :, :, :]).then_inc(S["span_ok"], 1)
            dve.wait_ge(S["consts"], 29)
            with dve.Fori(0, 4) as i:
                for k in range(4):
                    n, e = 4 * i + k, k % 2
                    dve.wait_ge(S["emb_tr"], n + 1)
                    if k > 1:
                        dve.wait_ge(S["emb_mm"], n - 1)
                    else:
                        dve.wait_ge(S["emb_mm"], n)
                    v.tensor_copy(eT2[0:C, e, :], PD[e][0:C, 0:500]).then_inc(S["emb_c2"], 1)
            dve.wait_ge(S["loads_q"], 18 * 16)
            step(v.tensor_scalar(mixes[C:P, 0:3], mixes[C:P, 0:3], -1.0, 1.0, ALU.mult, ALU.add))
            for n in range(3):
                v.tensor_scalar(w_mix[:, n * C:(n + 1) * C], w_mix[:, n * C:(n + 1) * C], mixes[:, n:n + 1],
                                None, ALU.mult).then_inc(S["mix_ok"], 1)
            dve.wait_ge(S["tgt_in"], 48)
            for r in range(ROUNDS):
                for m in range(8):
                    step(v.tensor_scalar(same, tgt_row[:, r], tg_f[:, r, m:m + 1], None, ALU.is_equal))
                    step(v.scalar_tensor_tensor(junk, later, float(m), same, op0=ALU.is_gt, op1=ALU.mult,
                                                accum_out=dup[:, r, m:m + 1]))
            step(v.tensor_scalar(dup[:, :, :], dup[:, :, :], 0.0, 1.0e6, ALU.is_gt, ALU.mult))
            step(v.tensor_tensor(tg_f[:, :, :], tg_f[:, :, :], dup[:, :, :], ALU.add))
            v.tensor_copy(tg_u[:, :, :], tg_f[:, :, :]).then_inc(S["dup_ok"], 1)
            for r in range(ROUNDS):
                dve.wait_ge(S["src_in"], 16 * 32 * (r + 1))
                v.tensor_tensor(src_t, src_t, sp_m[:, r, :, :, None].to_broadcast([P, 8, SPAN, C]),
                                ALU.mult).then_inc(S["masked"], 1)
                dve.wait_ge(S["masked"], r + 1)
                v.tensor_tensor(src_t[:, :, 0:2], src_t[:, :, 0:2], src_t[:, :, 2:4], ALU.add).then_inc(S["summed"], 1)
                dve.wait_ge(S["summed"], 2 * r + 1)
                v.tensor_tensor(mean_t, src_t[:, :, 0], src_t[:, :, 1], ALU.add).then_inc(S["summed"], 1)
                dve.wait_ge(S["summed"], 2 * r + 2)
                v.tensor_tensor(mean_t, mean_t, n_in[:, r, :, None].to_broadcast([P, 8, C]), ALU.mult).then_inc(
                    S["mean_ok"], 1)
                dve.wait_ge(S["mean_tr"], r + 1)
                v.tensor_copy(meanT[0:C, 0:512], XA[0:C, :]).then_inc(S["mean_c"], 1)
                dve.wait_ge(S["comp_mm"], r + 1)
                wait(dve, S["scat_ok"], 128 * r)
                v.tensor_copy(comp_t, XO[:, :].rearrange("p (g d) -> p g d", g=8)).then_inc(S["comp_ok"], 1)

            def chunk_mask(s, w):
                dve.wait_ge(S["exp_ready"], SLOTS * w + s + 1)
                if s >= 4:
                    dve.wait_ge(S["pv_done"], SLOTS * w + s - 3)
                else:
                    wait(dve, S["pv_done"], SLOTS * w)
                v.scalar_tensor_tensor(W[:, s % 4, :], PD[s % 2][:, :], float(TOPK), E[:, s % 2, :],
                                       op0=ALU.is_gt, op1=ALU.mult).then_inc(S["weights_ready"], 1)

            def front(s, b):
                if s == 2:
                    dve.wait_ge(S["h0_in"], 16 * (b + 1))
                    v.bn_stats(stats[:, :], h0[:, :]).then_inc(S["stat1_ok"], 1)
                if s == 3:
                    dve.wait_ge(S["stat1_ok"], b + 1)
                    fence()
                    v.bn_aggr(mv[:, :], stats[:, :]).then_inc(S["var1_ok"], 1)
                    dve.wait_ge(S["var1_ok"], b + 1)
                    v.tensor_scalar(vareps[:, :], mv[:, 1:2], EPS, None, ALU.add).then_inc(S["ve1_ok"], 1)
                if s == 5:
                    dve.wait_ge(S["rstd1_ok"], b + 1)
                    wait(dve, S["xn2_tr"], b)
                    v.tensor_scalar(xn2[:, :, :], h0[:, None, :].to_broadcast([P, 2, C]), mv[:, 0:1], rstd[:, :],
                                    ALU.subtract, ALU.mult).then_inc(S["xn2_ok"], 1)
                if s == 11:
                    dve.wait_ge(S["kvr_mm"], b + 1)
                    v.tensor_scalar(k_c[:, :], XA[:, 0:C], -60.0, 30.0, ALU.max, ALU.min).then_inc(S["kclip_ok"], 1)
                if s == 13:
                    dve.wait_ge(S["k_ok"], b + 1)
                    v.tensor_tensor(kv_t[:, :], k_e[:, :], XA[:, C:2 * C], ALU.mult).then_inc(S["kv_ok"], 1)
                if s == 15:
                    dve.wait_ge(S["scan_mm"], b + 1)
                    dve.wait_ge(S["er_ok"], b + 1)
                    v.scalar_tensor_tensor(den[:, :], e_r[:, :], 1.0, XA[:, 192:256], op0=ALU.add,
                                           op1=ALU.mult).then_inc(S["den_ok"], 1)
                if s == 16:
                    dve.wait_ge(S["den_ok"], b + 1)
                    v.reciprocal(rden[:, :], den[:, :]).then_inc(S["rden_ok"], 1)
                if s == 17:
                    dve.wait_ge(S["rden_ok"], b + 1)
                    v.tensor_tensor(rwkv[:, :], rden[:, :], XA[:, 256:320], ALU.mult).then_inc(S["rwkv_ok"], 1)
                if s == 21:
                    dve.wait_ge(S["proj_mm"], b + 1)
                    wait(dve, S["h1_w"], 16 * b)
                    v.tensor_tensor(h1[:, :], h0[:, :], XA[:, 448:512], ALU.add).then_inc(S["h1_ok"], 1)
                if s == 22:
                    dve.wait_ge(S["h1_ok"], b + 1)
                    v.bn_stats(stats[:, :], h1[:, :]).then_inc(S["stat2_ok"], 1)
                if s == 23:
                    dve.wait_ge(S["stat2_ok"], b + 1)
                    fence()
                    v.bn_aggr(mv[:, :], stats[:, :]).then_inc(S["var2_ok"], 1)
                    dve.wait_ge(S["var2_ok"], b + 1)
                    v.tensor_scalar(vareps[:, :], mv[:, 1:2], EPS, None, ALU.add).then_inc(S["ve2_ok"], 1)
                if s == 25:
                    dve.wait_ge(S["rstd2_ok"], b + 1)
                    v.tensor_scalar(xn[:, :], h1[:, :], mv[:, 0:1], rstd[:, :], ALU.subtract, ALU.mult).then_inc(
                        S["xn_ok"], 1)
                if 31 <= s <= 49:
                    k = s - 31
                    if k == 0:
                        dve.wait_ge(S["sim0_ok"], b + 1)
                        wait(dve, S["shifted_ok"], 2 * b)
                    if k == 2:
                        dve.wait_ge(S["sim1_ok"], b + 1)
                    if k == 1:
                        wait(dve, S["low_ok"], 2 * b)
                    if k > 0:
                        dve.wait_ge(S["topk_step"], 19 * b + k)
                    fence()
                    for g, st in ((k - 3, 3), (k - 2, 2), (k - 1, 1), (k, 0)):
                        if not 0 <= g < 2 * HEADS:
                            continue
                        side, h = g // HEADS, g % HEADS
                        if st == 0:
                            last = v.max(top[:, side, h, 0:8], sim[:, side, h, :])
                        if st == 1:
                            v.max_index(idx[:, side, h, 0:8], top[:, side, h, 0:8], sim[:, side, h, :])
                            last = v.match_replace(simr[:, side, h, :], top[:, side, h, 0:8], sim[:, side, h, :], NEG)
                        if st == 2:
                            last = v.max(top[:, side, h, 8:16], simr[:, side, h, :])
                        if st == 3:
                            last = v.max_index(idx[:, side, h, 8:16], top[:, side, h, 8:16], simr[:, side, h, :])
                    last.then_inc(S["topk_step"], 1)
                if s in (49, 50):
                    v0, v1 = top[:, 0], top[:, 1]
                    if s == 49:
                        dve.wait_ge(S["topk_step"], 19 * (b + 1))
                        for r_ in range(3):
                            v.tensor_tensor(cand[:, :, STARTS[r_]:STARTS[r_] + RUNS[r_]],
                                            v0[:, :, r_:r_ + 1].to_broadcast([P, HEADS, RUNS[r_]]),
                                            v1[:, :, 0:RUNS[r_]], ALU.add)
                        v.tensor_copy(idx_b[:, :, :, :], idx[:, :, :, :]).then_inc(S["idxb_ok"], 1)
                    else:
                        for r_ in (3, 4):
                            v.tensor_tensor(cand[:, :, STARTS[r_]:STARTS[r_] + RUNS[r_]],
                                            v0[:, :, r_:r_ + 1].to_broadcast([P, HEADS, RUNS[r_]]),
                                            v1[:, :, 0:RUNS[r_]], ALU.add)
                        v.tensor_tensor(cand[:, :, STARTS[5]:STARTS[8]].rearrange("p h (a b) -> p h a b", b=2),
                                        v0[:, :, 5:8, None].to_broadcast([P, HEADS, 3, 2]),
                                        v1[:, :, None, 0:2].to_broadcast([P, HEADS, 3, 2]), ALU.add)
                        v.tensor_tensor(cand[:, :, STARTS[8]:], v0[:, :, 8:16],
                                        v1[:, :, 0:1].to_broadcast([P, HEADS, 8]), ALU.add).then_inc(S["cand_ok"], 1)
                if 51 <= s <= 57:
                    k = s - 51
                    if k == 0:
                        dve.wait_ge(S["cand_ok"], b + 1)
                        v.tensor_tensor(expd[:, :, :], cand[:, :, :], cand[:, :, 0:1].to_broadcast([P, HEADS, PAIRS]),
                                        ALU.subtract).then_inc(S["gap_ok"], 1)
                    else:
                        dve.wait_ge(S["stair_step"], 7 * b + k)
                        fence()
                    for g, st in ((k - 3, 3), (k - 2, 2), (k - 1, 1), (k, 0)):
                        if not 0 <= g < HEADS // 2:
                            continue
                        for h in (2 * g, 2 * g + 1):
                            if st == 0:
                                last = v.max(top_a[:, h, :], cand[:, h, :])
                            if st == 1:
                                last = v.match_replace(candr[:, h, :], top_a[:, h, :], cand[:, h, :], NEG)
                            if st == 2:
                                last = v.max(top_b[:, h, :], candr[:, h, :])
                            if st == 3:
                                last = v.match_replace(picked[:, h, :], top_b[:, h, :], candr[:, h, :], NEG)
                    last.then_inc(S["stair_step"], 1)
                if s == 58:
                    dve.wait_ge(S["stair_step"], 7 * (b + 1))
                    v.tensor_scalar(picked[:, :, :], picked[:, :, :], NEG / 2, None, ALU.is_lt).then_inc(
                        S["picked_ok"], 1)
                if s == 59:
                    dve.wait_ge(S["picked_ok"], b + 1)
                    dve.wait_ge(S["expd_ok"], b + 1)
                    v.tensor_tensor(expd[:, :, :], expd[:, :, :], picked[:, :, :], ALU.mult).then_inc(
                        S["weighed_ok"], 1)
                if s == 60:
                    dve.wait_ge(S["weighed_ok"], b + 1)
                    v.tensor_reduce(zsum[:, :], expd[:, :, :], AX.X, ALU.add).then_inc(S["z_ok"], 1)
                with nc.allow_low_precision(reason="counts up to 16 are exact in bf16"):
                    if s == 61:
                        for r_ in range(3):
                            v.tensor_reduce(count[:, :, r_:r_ + 1], picked[:, :, STARTS[r_]:STARTS[r_] + RUNS[r_]],
                                            AX.X, ALU.add)
                    if s == 62:
                        for r_ in (3, 4):
                            v.tensor_reduce(count[:, :, r_:r_ + 1], picked[:, :, STARTS[r_]:STARTS[r_] + RUNS[r_]],
                                            AX.X, ALU.add)
                    if s == 63:
                        v.tensor_reduce(count[:, :, 5:8], picked[:, :, STARTS[5]:STARTS[8]].rearrange(
                            "p h (a b) -> p h a b", b=2), AX.X, ALU.add)
                        v.tensor_copy(count[:, :, 8:16], picked[:, :, STARTS[8]:]).then_inc(S["count_ok"], 1)
                if s == 63:
                    dve.wait_ge(S["lnz_ok"], b + 1)
                    v.tensor_tensor(shift0[:, :], top[:, 0, :, 0], lnz[:, :], ALU.add).then_inc(S["shift_ok"], 1)

            def tail(s, t):
                if s < 8:
                    side, h = s // 4, 2 * (s % 4)
                    if s == 0:
                        dve.wait_ge(S["idxb_ok"], t + 1)
                        wait(dve, S["tree0_step"], 5 * t)
                    for hh in (h, h + 1):
                        last = v.tensor_tensor(hot[:, side, hh], idx_b[:, side, hh, None, :].to_broadcast(
                            [P, KEYS, TOPK]), key_no[:, :, :], ALU.is_equal)
                    last.then_inc(S[f"hot{side}_ok"], 1)
                if 8 <= s < 12:
                    h = 2 * (s - 8)
                    dve.wait_ge(S["hot1_ok"], 4 * t + s - 7)
                    for hh in (h, h + 1):
                        last = v.tensor_tensor(hot[:, 1, hh], hot[:, 1, hh],
                                               rank_w[:, None, :].to_broadcast([P, KEYS, TOPK]), ALU.mult)
                    last.then_inc(S["weigh1_ok"], 1)
                for side, base in ((1, 12), (0, 18)):
                    if base <= s < base + 5:
                        k = s - base
                        st = S[f"tree{side}_step"]
                        if k in (0, 1):
                            if side == 1:
                                dve.wait_ge(S["weigh1_ok"], 4 * t + 2 * k + 2)
                            else:
                                dve.wait_ge(S["weigh0_ok"], HEADS * t + 4 * k + 4)
                            for hh in range(4 * k, 4 * k + 4, 2):
                                x_ = hot[:, side, hh:hh + 2]
                                last = v.tensor_tensor(x_[:, :, :, 0:8], x_[:, :, :, 0:8], x_[:, :, :, 8:16], ALU.add)
                            last.then_inc(st, 1)
                        elif k in (2, 3):
                            n = (4, 2)[k - 2]
                            dve.wait_ge(st, 5 * t + k)
                            x_ = hot[:, side]
                            v.tensor_tensor(x_[:, :, :, 0:n], x_[:, :, :, 0:n], x_[:, :, :, n:2 * n],
                                            ALU.add).then_inc(st, 1)
                        else:
                            dve.wait_ge(st, 5 * t + k)
                            wait(dve, S["rows_tr"], 4 * t)
                            pt, n = ((parts0, CI), (parts1, CJ))[side]
                            x_ = hot[:, side].rearrange("p h (g i) a -> p h g i a", i=n)
                            v.tensor_tensor(pt[:, :, :, 3, :], x_[:, :, :, :, 0], x_[:, :, :, :, 1],
                                            ALU.add).then_inc(st, 1)

            def attend(s, c):
                for hg, base in ((0, 38), (1, 50)):
                    n = 2 * c + hg
                    if s == base + 3:
                        dve.wait_ge(S["att_mm"], n + 1)
                        wait(dve, S["att_tr"], n)
                        v.scalar_tensor_tensor(att[:, :, :], XC[:, :].rearrange("p (h t) -> p h t", h=4), C ** -0.5,
                                               causal[:, None, :].to_broadcast([P, 4, T]), op0=ALU.mult,
                                               op1=ALU.add).then_inc(S["masked_ok"], 1)
                    if s == base + 4:
                        dve.wait_ge(S["masked_ok"], n + 1)
                        v.tensor_reduce(nmax[:, :], att[:, :, :], AX.X, ALU.max, negate=True).then_inc(
                            S["nmax_ok"], 1)
                    if s == base + 7:
                        dve.wait_ge(S["aexp_ok"], 4 * (n + 1))
                        v.reciprocal(rsum[:, :], asum[:, :]).then_inc(S["rsum_ok"], 1)
                    if s == base + 8:
                        dve.wait_ge(S["rsum_ok"], n + 1)
                        v.tensor_tensor(att[:, :, :], att[:, :, :], rsum[:, :, None].to_broadcast([P, 4, T]),
                                        ALU.mult).then_inc(S["att_ok"], 1)
                    if s == base + 13:
                        dve.wait_ge(S["o_mm"], n + 1)
                        if hg == 0:
                            wait(dve, S["out_w"], 16 * c)
                        else:
                            dve.wait_ge(S["res_ok"], n)
                        v.tensor_tensor(res[:, :], (h1_c, res)[hg][:, :], XO[:, 256:256 + C], ALU.add).then_inc(
                            S["res_ok"], 1)

            def window(t, F, Tl, Bb, Cc, first=False, last=False):
                w = t - 4
                for s in range(SLOTS):
                    if Bb:
                        chunk_mask(s, w)
                    if Tl:
                        tail(s, t)
                    if F:
                        front(s, t + 1)
                    if Cc:
                        attend(s, t - 8)
            run_windows(dve, window)


LAG_B, LAG_C = 4, 8


def run_windows(eng, window):
    window(-1, True, False, False, False)
    with eng.Fori(0, 3) as t:
        window(t, True, True, False, False)
    window(3, True, True, False, False, first=True)
    with eng.Fori(4, 8) as t:
        window(t, True, True, True, False)
    with eng.Fori(8, B - 1) as t:
        window(t, True, True, True, True)
    window(B - 1, False, True, True, True)
    with eng.Fori(B, B + 3) as t:
        window(t, False, False, True, True)
    window(B + 3, False, False, True, True, last=True)
    with eng.Fori(B + 4, B + 8) as t:
        window(t, False, False, False, True)


_INS = ["x", "L0_tok_spans0", "L0_tok_spans1", "L0_tok_spans2", "L0_tok_emb_table", "L0_tok_w_down",
        "L0_tok_b_down", "L0_tok_wc1", "L0_tok_bc1", "L0_tok_wc2", "L0_tok_bc2", "L0_attn_time_w",
        "L0_attn_time_mix_k", "L0_attn_time_mix_v", "L0_attn_time_mix_r", "L0_attn_Wk", "L0_attn_Wv",
        "L0_attn_Wr", "L0_attn_Wo", "L0_ffn_Wq_pk", "L0_ffn_pk_keys", "L0_ffn_Wq", "L0_ffn_keys_table",
        "L0_ffn_values_table", "L0_ffn_Wo"]


def kernel(**inputs):
    import concourse.bacc as bacc
    from concourse.bass_utils import run_bass_kernel_spmd
    arrays = {f"in_{n}": np.ascontiguousarray(inputs[n]) for n in _INS}
    nc = bacc.Bacc("TRN2", target_bir_lowering=False, num_devices=1)
    args = [nc.dram_tensor(f"in_{n}", arrays[f"in_{n}"].shape, mybir.dt.from_np(arrays[f"in_{n}"].dtype),
                           kind="ExternalInput").ap() for n in _INS]
    out = nc.dram_tensor("out_h", (B, T, C), F32, kind="ExternalOutput").ap()
    tower(nc, *args, out)
    r = run_bass_kernel_spmd(nc, [arrays], core_ids=[0])
    return r.results[0]["out_h"]
```

```python
from contextlib import ExitStack

import concourse.bass as bass
from concourse import mybir
import numpy as np

F32 = mybir.dt.float32
BF16 = mybir.dt.bfloat16
I32 = mybir.dt.int32
U32 = mybir.dt.uint32
ALU = mybir.AluOpType
ACT = mybir.ActivationFunctionType
AX = mybir.AxisListType

P = 128
B, T, C = 128, 128, 64
N_TOK = B * T
VOCAB, D_EMB = 8000, 192
N_SPAN, SPAN, ROUNDS = 1024, 4, 3
PAD = -100.0
EPS = 1e-5
HEADS, KEYS, TOPK = 8, 64, 16
NUM_KV = KEYS * KEYS
D_KEY = 32
TIME_LEN = 512
NEG = -3.0e38
MASKED = -1.0e30

BLOCK = 4
BT = BLOCK * T
UNITS = (B // BLOCK) * HEADS
CI, CJ = 16, 8
NI, NJ = KEYS // CI, KEYS // CJ
CHUNKS = NI * NJ
SLOTS = 2 * CHUNKS
SIDE0_ROWS, SIDE1_ROWS = 4 * CI, 4 * CJ
ROWS = SIDE0_ROWS + SIDE1_ROWS
SIDE_ROWS = 4 * KEYS
HOT_SLOTS = (2, 3, 4, 5, 6, 7, 7, 8, 9, 9, 10, 11, 12, 13, 14, 15)
POOL_WEIGHS = (16, 17, 18, 25)
DVE_WEIGHS = HEADS - len(POOL_WEIGHS)
TREE = 7
TREE_SLOTS = {20: ((0, 0),), 21: ((0, 1),), 22: ((0, 2),), 23: ((0, 3),), 24: ((0, 4),), 25: ((0, 5),),
              26: ((0, 6),), 27: ((1, 0),), 28: ((1, 1),), 29: ((1, 2), (1, 3)), 30: ((1, 4),),
              31: ((1, 5),), 32: ((1, 6),)}
LOAD_UNIT = 16 * (NI + NJ + 1)

RUNS = [TOPK // (a + 1) for a in range(TOPK)]
STARTS = [sum(RUNS[:a]) for a in range(TOPK)]
PAIRS = sum(RUNS)


def wait(eng, sem, value):
    if isinstance(value, int) and value <= 0:
        return
    eng.wait_ge(sem, value)


def tower(nc, x, spans0, spans1, spans2, emb_table, w_down, b_down, wc1, bc1, wc2, bc2,
          time_w, mix_k, mix_v, mix_r, Wk, Wv, Wr, Wo, Wq_pk, pk_keys, Wq, keys_table,
          values_table, Wo_ffn, out):
    ctx = ExitStack()
    with ctx:
        def sb(name, shape, dt):
            return ctx.enter_context(nc.sbuf_tensor(name, shape, dt))

        def pb(name):
            return ctx.enter_context(nc.psum_tensor(name, [P, 512], F32))

        def sem(name):
            return ctx.enter_context(nc.semaphore(name))

        def dram(name, shape, dt):
            return nc.dram_tensor(name, shape, dt, kind="Internal").ap()

        buf_d = dram("buf_d", (N_TOK, C), F32)
        tgt_d = dram("tgt_d", (ROUNDS, N_SPAN), F32)
        tw_d = dram("tw_d", (2, T), F32)
        tab_d = dram("tab_d", (HEADS, P, CHUNKS, P), F32)
        rows_d = dram("rows_d", (UNITS, 2 * SIDE_ROWS, BT), BF16)
        kv_d = dram("kv_d", (UNITS, P, BT), F32)
        h1_d = dram("h1_d", (B, T, C), F32)
        xn_d = dram("xn_d", (B, C, T), F32)

        combo_s = sb("combo_s", [P, 2 * CHUNKS * BT // 2], F32)
        table_s = sb("table_s", [P, 2 * CHUNKS * P], F32)
        hot_s = sb("hot_s", [P, 2 * HEADS * KEYS * TOPK // 2], F32)
        parts_s = sb("parts_s", [P, HEADS * 2 * SIDE_ROWS // 2], F32)
        rowsT_s = sb("rowsT_s", [P, 32 * P // 2], F32)
        combo = combo_s[:, :].bitcast(BF16).rearrange("p (k c t) -> p k c t", k=2, c=CHUNKS)
        table = table_s[:, :].rearrange("p (k c d) -> p k c d", k=2, c=CHUNKS)
        hot = hot_s[:, :].bitcast(BF16).rearrange("p (s h i a) -> p s h i a", s=2, h=HEADS, i=KEYS)
        parts = parts_s[:, :].bitcast(BF16)
        parts0 = parts.rearrange("p (h s r) -> p h s r", h=HEADS, s=2)[:, :, 0, :].rearrange(
            "p h (g q i) -> p h g q i", g=NI, q=4)
        parts1 = parts.rearrange("p (h s r) -> p h s r", h=HEADS, s=2)[:, :, 1, :].rearrange(
            "p h (g q i) -> p h g q i", g=NJ, q=4)
        rowsT = rowsT_s[:, :].bitcast(BF16)

        emb_t = combo_s[:, 0:4 * 4 * D_EMB].rearrange("p (k j d) -> p k j d", k=4, j=4)
        eT1 = combo_s[:, 4096:4096 + 4 * P]
        eT2 = combo_s[:, 5120:5120 + 4 * P]
        src_t = combo_s[:, 8192:8192 + 2048].rearrange("p (g s d) -> p g s d", g=8, s=SPAN)
        mean_t = combo_s[:, 10240:10240 + 512].rearrange("p (g d) -> p g d", g=8)
        meanT = combo_s[:, 10752:10752 + 1024]
        hidT = combo_s[:, 11776:11776 + 2048].rearrange("p (m n) -> p m n", m=2)
        comp_t = combo_s[:, 13824:13824 + 512].rearrange("p (g d) -> p g d", g=8)
        tgt_row = hot_s[:, 0:ROUNDS * N_SPAN].rearrange("p (r n) -> p r n", r=ROUNDS)
        later = hot_s[:, 3072:3072 + 1024]
        same = parts_s[:, 0:1024]
        junk = parts_s[:, 1024:2048]

        id_f = sb("id_f", [P, P], F32)
        id_b = sb("id_b", [P, P], BF16)
        flip = combo_s[:, 14336:14336 + P]
        triT = sb("triT", [P, P], F32)
        toepT = sb("toepT", [P, P], F32)
        toep_raw = combo_s[:, 14464:14464 + P]
        toep_mid = combo_s[:, 14592:14592 + P]
        causal = sb("causal", [P, P], F32)
        sel_s = sb("sel_s", [ROWS, P], BF16)
        sel_d = sb("sel_d", [ROWS, P], BF16)
        key_no = sb("key_no", [P, KEYS, TOPK], BF16)
        rank_w = sb("rank_w", [P, TOPK], BF16)
        half = sb("half", [P, 1], F32)
        fence_t = sb("fence_t", [P, 2], F32)
        wd1 = combo_s[:, 14720:14720 + C]
        wd2 = combo_s[:, 14784:14784 + C]
        wc1_t = combo_s[:, 14848:14848 + 256]
        wc2_t = combo_s[:, 15104:15104 + 128].rearrange("p (m n) -> p m n", m=2)
        ones_r = combo_s[:, 15232:15232 + P]
        bc2_t = combo_s[:, 15360:15360 + C]
        pkq = table_s[:, 0:512]
        keys_t = table_s[:, 512:1024]
        pkqT = table_s[:, 1024:1280].rearrange("p (k c) -> p k c", k=4)
        keysT = table_s[:, 1280:1536].rearrange("p (k c) -> p k c", k=4)
        rowbuf = table_s[:, 0:N_TOK * C // P]
        w_mix = sb("w_mix", [P, 3 * C], F32)
        mixes = sb("mixes", [P, 4], F32)
        wo_a = sb("wo_a", [C, C], F32)
        pk_m = sb("pk_m", [C, 2 * HEADS * KEYS], F32)
        wq_t = sb("wq_t", [C, HEADS * C], F32)
        wo_f = sb("wo_f", [P, HEADS, C], F32)
        ids_i = combo_s[:, 15424:15424 + P].bitcast(I32)
        ids_f = combo_s[:, 15552:15552 + P]
        ids_n = combo_s[:, 15680:15680 + P]
        ids_u = combo_s[:, 15808:15808 + P].bitcast(U32)
        sp_i = combo_s[:, 15936:15936 + 96].bitcast(I32).rearrange("p (r m s) -> p r m s", r=ROUNDS, m=8)
        sp_f = combo_s[:, 16032:16032 + 96].rearrange("p (r m s) -> p r m s", r=ROUNDS, m=8)
        sp_n = combo_s[:, 16128:16128 + 96].rearrange("p (r m s) -> p r m s", r=ROUNDS, m=8)
        sp_u = combo_s[:, 16224:16224 + 96].bitcast(U32).rearrange("p (r m s) -> p r m s", r=ROUNDS, m=8)
        sp_m = sb("sp_m", [P, ROUNDS, 8, SPAN], F32)
        tg_f = sb("tg_f", [P, ROUNDS, 8], F32)
        tg_n = sb("tg_n", [P, ROUNDS, 8], F32)
        tg_u = sb("tg_u", [P, ROUNDS, 8], U32)
        dup = sb("dup", [P, ROUNDS, 8], F32)
        n_in = sb("n_in", [P, ROUNDS, 8], F32)

        E = sb("E", [P, 2, BT], F32)
        W = sb("W", [P, 4, BT], F32)
        kv_out = sb("kv_out", [P, 2, BT], F32)
        h0 = sb("h0", [P, C], F32)
        stats = sb("stats", [P, 6], F32)
        mv = sb("mv", [P, 2], F32)
        rstd = sb("rstd", [P, 1], F32)
        vareps = sb("vareps", [P, 1], F32)
        xn2 = sb("xn2", [P, 2, C], F32)
        xxT = sb("xxT", [P, T], F32)
        k_e = sb("k_e", [P, C], F32)
        k_c = sb("k_c", [P, C], F32)
        kv_t = sb("kv_t", [P, C], F32)
        e_r = sb("e_r", [P, C], F32)
        den = sb("den", [P, C], F32)
        rden = sb("rden", [P, C], F32)
        rwkv = sb("rwkv", [P, C], F32)
        rwT = sb("rwT", [C, T], F32)
        h1 = sb("h1", [P, C], F32)
        xn = sb("xn", [P, C], F32)
        xnT = sb("xnT", [C, T], F32)
        sim = sb("sim", [P, 2, HEADS, KEYS], F32)
        simr = sb("simr", [P, 2, HEADS, KEYS], F32)
        top = sb("top", [P, 2, HEADS, TOPK], F32)
        idx = sb("idx", [P, 2, HEADS, TOPK], U32)
        idx_b = sb("idx_b", [P, 2, HEADS, TOPK], BF16)
        cand = sb("cand", [P, HEADS, PAIRS], F32)
        candr = sb("candr", [P, HEADS, PAIRS], F32)
        picked = cand
        expd = sb("expd", [P, HEADS, PAIRS], F32)
        top_a = sb("top_a", [P, HEADS, 8], F32)
        top_b = sb("top_b", [P, HEADS, 8], F32)
        zsum = sb("zsum", [P, HEADS], F32)
        lnz = sb("lnz", [P, HEADS], F32)
        shift0 = sb("shift0", [P, HEADS], F32)
        count = sb("count", [P, HEADS, TOPK], BF16)
        resid = simr
        kv_c = sb("kv_c", [P, HEADS, T], F32)
        xnT_c = sb("xnT_c", [C, T], F32)
        h1_c = sb("h1_c", [P, C], F32)
        qT = sb("qT", [C, 4, T], F32)
        att = sb("att", [P, 4, T], F32)
        attT = sb("attT", [P, 4, T], F32)
        vo = sb("vo", [P, 4, C], F32)
        nmax = sb("nmax", [P, 4], F32)
        asum = sb("asum", [P, 4], F32)
        rsum = sb("rsum", [P, 4], F32)
        res = sb("res", [P, C], F32)

        PS = [pb("ps_s0"), pb("ps_s1")]
        PD = [pb("ps_d0"), pb("ps_d1")]
        PO = pb("ps_o")
        XA = pb("ps_a")
        XC = pb("ps_c")
        XO = pb("ps_x")
        XAb = XA[:, :].bitcast(BF16)

        names = """loads_w loads_p loads_q loads_x loads_sp emb_in0 emb_in1 emb_in2 emb_in3 emb_tr
        emb_c1 emb_c2 emb_mm emb_out consts ids_ok sp_ok span_ok tw_w tw_in tgt_w
        tgt_in dup_ok buf_w src_in0 src_in1 masked summed mean_ok mean_tr mean_c hid_mm hid_ok comp_mm
        comp_ok scat_ok prep_step pk_tr pk_c pk_step pk_ok mix_ok toep_tr toep_c toep_mm toep_ok
        tab_w combo_in0 combo_in1 scores_ready test_ready exp_ready weights_ready pv_done kv_ready kv_w0 kv_w1
        h0_in var1_ok rstd1_ok xn2_ok xn2_tr xxT_ok kvr_mm kclip_ok er_ok k_ok kv_ok scan_mm den_ok
        rden_ok rwkv_ok rw_tr rwT_ok proj_mm h1_ok stat1_ok stat2_ok var2_ok rstd2_ok xn_ok xn_tr xnT_ok h1_w xn_w
        sim0_mm sim0_ok sim1_mm sim1_ok topk_step idxb_ok cand_ok gap_ok expd_ok stair_step
        picked_ok weighed_ok z_ok lnz_ok shift_ok count_ok shifted_ok high_ok resid_ok mid_ok low_ok
        hot0_ok hot1_ok weigh0_ok weigh1_ok weigh1_pool tree1_step tree0_step rows_tr rows_c rows_w c_in q_mm q_ok
        att_mm vo_mm vo_ok masked_ok nmax_ok aexp_ok rsum_ok att_ok att_tr attT_ok o_mm res_ok out_w
        fence_v ve1_ok ve2_ok""".split()
        S = {n: sem(n) for n in names}
        block = ctx.enter_context(nc.Block())

        sp_src = [s.rearrange("(p g) s -> p g s", g=8) for s in (spans0, spans1, spans2)]
        keys_v = keys_table.rearrange("(h g j i2 i) d -> h j i g i2 d", h=HEADS, g=NJ, j=CJ, i2=NI)
        vals_v = values_table.rearrange("(h g j i2 i) d -> h j i g i2 d", h=HEADS, g=NJ, j=CJ, i2=NI)

        @block.sync
        def _(sp):
            sp.dma_start(ids_i, x).then_inc(S["loads_x"], 16)
            for r in range(ROUNDS):
                sp.dma_start(sp_i[:, r], sp_src[r]).then_inc(S["loads_sp"], 16)
            sp.dma_start(wd1, w_down[0:P, :]).then_inc(S["loads_w"], 16)
            sp.dma_start(wd2[0:C], w_down[P:D_EMB, :]).then_inc(S["loads_w"], 16)
            sp.dma_start(wd2[C:C + 1], b_down[None, :]).then_inc(S["loads_w"], 16)
            sp.dma_start(wc1_t[0:C], wc1).then_inc(S["loads_p"], 16)
            sp.dma_start(wc1_t[C:C + 1], bc1[None, :]).then_inc(S["loads_p"], 16)
            sp.dma_start(wc2_t, wc2.rearrange("(m k) n -> k m n", m=2)).then_inc(S["loads_p"], 16)
            sp.dma_start(bc2_t[0:1], bc2[None, :]).then_inc(S["loads_p"], 16)
            for lo in (0, C):
                for n, w in enumerate((Wk, Wv, Wr)):
                    sp.dma_start(w_mix[lo:lo + C, n * C:(n + 1) * C], w).then_inc(S["loads_q"], 16)
                for n, m in enumerate((mix_k, mix_v, mix_r)):
                    with nc.allow_non_contiguous_dma(reason="64 channel weights, once"):
                        sp.dma_start(mixes[lo:lo + C, n:n + 1], m.rearrange("a b c -> (a b) c").rearrange(
                            "a c -> c a")).then_inc(S["loads_q"], 16)
            sp.dma_start(wo_a[:, :], Wo).then_inc(S["loads_q"], 16)
            sp.dma_start(wq_t[:, :], Wq).then_inc(S["loads_q"], 16)
            sp.dma_start(wo_f[C:P], Wo_ffn.rearrange("(h d) n -> d h n", h=HEADS)).then_inc(S["loads_q"], 16)
            sp.dma_start(pkq[0:C], Wq_pk).then_inc(S["loads_q"], 16)
            for p_ in range(2):
                sp.dma_start(keys_t[0:C, p_ * 256:(p_ + 1) * 256],
                             pk_keys[p_].rearrange("k h d -> k (h d)")).then_inc(S["loads_q"], 16)
            sp.dma_start(tw_d[0:1, :], time_w[None, TIME_LEN - T:]).then_inc(S["tw_w"], 16)
            sp.wait_ge(S["consts"], 16)
            sp.dma_start(tw_d[1:2, :], junk[0:1, 0:T]).then_inc(S["tw_w"], 16)
            sp.wait_ge(S["tw_w"], 32)
            tw_rows = bass.AP(tensor=tw_d.tensor, offset=0, ap=[[1, P], [1, P]])
            sp.dma_start(toep_raw, tw_rows).then_inc(S["tw_in"], 16)
            sp.wait_ge(S["sp_ok"], 1)
            for r in range(ROUNDS):
                sp.dma_start(tgt_d[r].rearrange("(p g) -> p g", g=8), tg_f[:, r]).then_inc(S["tgt_w"], 16)
            sp.wait_ge(S["tgt_w"], 16 * ROUNDS)
            for r in range(ROUNDS):
                sp.dma_start(tgt_row[:, r], tgt_d[r:r + 1, :].to_broadcast([P, N_SPAN])).then_inc(
                    S["tgt_in"], 16)
            def order_tables(lo, hi):
                with sp.Fori(lo, hi) as h:
                    for kv, tab in enumerate((keys_v, vals_v)):
                        for j in range(CJ):
                            for i2 in range(NI):
                                sp.dma_start(
                                    tab_d[h, j * CI:(j + 1) * CI].rearrange(
                                        "i (g i2) d -> i g i2 d", i2=NI)[:, :, i2, kv * C:(kv + 1) * C],
                                    tab[h, j, :, :, i2, :]).then_inc(S["tab_w"], 16)

            order_tables(0, HEADS // 2)
            sp.wait_ge(S["emb_out"], P // 4)
            sp.dma_start(buf_d.rearrange("(p j) d -> p (j d)", p=P), rowbuf).then_inc(S["buf_w"], 16)
            order_tables(HEADS // 2, HEADS)

            def snap(value):
                return value if isinstance(value, int) else sp.snap(value)

            def load_unit(u, head, k, done, rows):
                wait(sp, S["pv_done"], done)
                sp.wait_ge(S["rows_w"], rows)
                for g in range(NI):
                    src = rows_d[u, g * SIDE0_ROWS:(g + 1) * SIDE0_ROWS, :]
                    dst = combo[0:SIDE0_ROWS, k].rearrange("p (gj gi) t -> p gj gi t", gi=NI)[:, :, g, :]
                    sp.dma_start(dst, src[:, None, :].to_broadcast([SIDE0_ROWS, NJ, BT])).then_inc(
                        S[f"combo_in{k}"], 16)
                for g in range(NJ):
                    src = rows_d[u, SIDE_ROWS + g * SIDE1_ROWS:SIDE_ROWS + (g + 1) * SIDE1_ROWS, :]
                    sp.dma_start(combo[SIDE0_ROWS:ROWS, k, g * NI:(g + 1) * NI, :],
                                 src[:, None, :].to_broadcast([SIDE1_ROWS, NI, BT])).then_inc(
                        S[f"combo_in{k}"], 16)
                sp.dma_start(table[:, k], tab_d[head]).then_inc(S[f"combo_in{k}"], 16)

            def store_unit(u, k):
                sp.wait_ge(S["kv_ready"], u + 1)
                sp.dma_start(kv_d[bass.ds(u, 1)].rearrange("a p t -> (a p) t"), kv_out[:, k, :]).then_inc(
                    S[f"kv_w{k}"], 16)

            def window(t, F, Tl, Bb, Cc, first=False, opening=False, last=False):
                b, w, c = t + 1, t - 4, t - 8
                done1, done2 = SLOTS * w, SLOTS * w + CHUNKS
                rows1, rows2 = 16 * w + 16, 16 * t + 16 if Tl else 16 * B
                tb, tq = snap(t // BLOCK), snap(t % BLOCK)
                head1, head2 = snap((2 * t + 1) % HEADS), snap((2 * t + 2) % HEADS)
                if F and isinstance(b, int) and b == 0:
                    sp.wait_ge(S["scat_ok"], ROUNDS * 8 * 16)
                    sp.dma_start(h0[:, :], buf_d[0:T, :]).then_inc(S["h0_in"], 16)
                if Bb and not opening:
                    store_unit(2 * w - 1, 1)
                if Cc:
                    wait(sp, S["res_ok"], 2 * c)
                    for k in range(2):
                        sp.wait_ge(S[f"kv_w{k}"], 8 * (2 * t - 8) if Bb else 8 * UNITS)
                    sp.dma_start(kv_c[:, :, :], kv_d[bass.ds((tb - 2) * HEADS, HEADS), :, bass.ds(tq * T, T)].rearrange(
                        "h p t -> p h t")).then_inc(S["c_in"], 16)
                    sp.wait_ge(S["h1_w"], 16 * (c + 1))
                    sp.wait_ge(S["xn_w"], 16 * (c + 1))
                    sp.dma_start(h1_c[:, :], h1_d[bass.ds(c, 1)].rearrange("a t c -> (a t) c")).then_inc(S["c_in"], 16)
                    sp.dma_start(xnT_c[:, :], xn_d[bass.ds(c, 1)].rearrange("a c t -> (a c) t")).then_inc(S["c_in"], 16)
                if Bb:
                    load_unit(2 * w + 1, head1, 1, done1, rows1)
                if F:
                    sp.wait_ge(S["h1_ok"], b + 1)
                    nb = snap((b + 1) % B)
                    sp.dma_start(h0[:, :], buf_d[bass.ds(nb * T, T), :]).then_inc(S["h0_in"], 16)
                    sp.dma_start(h1_d[bass.ds(b, 1)].rearrange("a t c -> (a t) c"), h1[:, :]).then_inc(S["h1_w"], 16)
                    sp.wait_ge(S["xnT_ok"], b + 1)
                    sp.dma_start(xn_d[bass.ds(b, 1)].rearrange("a c t -> (a c) t"), xnT[:, :]).then_inc(S["xn_w"], 16)
                if Bb:
                    store_unit(2 * w, 0)
                if Tl:
                    sp.wait_ge(S["rows_c"], 4 * (t + 1))
                    dst = rows_d[bass.ds(tb * HEADS, HEADS), :, bass.ds(tq * T, T)].rearrange(
                        "h (k p) t -> p (h k) t", p=P)
                    sp.dma_start(dst, rowsT.rearrange("p (k t) -> p k t", t=T)).then_inc(S["rows_w"], 16)
                if (Bb and not last) or first:
                    if first:
                        sp.wait_ge(S["tab_w"], 16 * HEADS * 2 * CJ * NI)
                        sp.wait_ge(S["pk_ok"], 2)
                    load_unit(2 * w + 2, head2, 0, done2 if Bb else 0, rows2)
                if Cc:
                    sp.wait_ge(S["res_ok"], 2 * c + 2)
                    sp.dma_start(out[bass.ds(c, 1)].rearrange("a t c -> (a t) c"), res[:, :]).then_inc(S["out_w"], 16)
                if last:
                    store_unit(2 * w + 1, 1)

            run_windows(sp, window)
            sp.wait_ge(S["out_w"], 16 * B)
            for k in range(2):
                sp.wait_ge(S[f"kv_w{k}"], 8 * UNITS)
            sp.wait_ge(S["rows_w"], 16 * B)
            sp.wait_ge(S["h1_w"], 16 * B)
            sp.wait_ge(S["xn_w"], 16 * B)

        @block.gpsimd
        def _(pool):
            g = nc.gpsimd
            cs = S["consts"]
            g.memset(id_f[:, :], 0.0).then_inc(cs, 1)
            g.memset(id_b[:, :], 0.0).then_inc(cs, 1)
            g.memset(flip, 0.0).then_inc(cs, 1)
            g.memset(triT[:, :], 1.0).then_inc(cs, 1)
            g.memset(causal[:, :], 0.0).then_inc(cs, 1)
            g.memset(sel_s[:, :], 0.0).then_inc(cs, 1)
            g.memset(sel_d[:, :], 0.0).then_inc(cs, 1)
            g.memset(half[:, :], -0.5).then_inc(cs, 1)
            g.memset(junk[:, 0:T], 0.0).then_inc(cs, 1)
            g.memset(ones_r, 1.0).then_inc(cs, 1)
            g.memset(xxT[:, :], 0.0).then_inc(cs, 1)
            for n, m in enumerate((eT2[C:C + 1], meanT[C:C + 1])):
                pool.wait_ge(cs, 11 + n)
                g.memset(m, 1.0).then_inc(cs, 1)
            pool.wait_ge(cs, 13)
            g.iota(key_no[:, :, :], [[1, KEYS], [0, TOPK]], base=0, channel_multiplier=0,
                   allow_small_or_imprecise_dtypes=True).then_inc(cs, 1)
            g.iota(rank_w[:, :], [[-1, TOPK]], base=TOPK, channel_multiplier=0,
                   allow_small_or_imprecise_dtypes=True).then_inc(cs, 1)
            g.iota(later, [[1, N_SPAN]], base=0, channel_multiplier=-8,
                   allow_small_or_imprecise_dtypes=True).then_inc(cs, 1)
            pool.wait_ge(cs, 16)
            for m, base, step, op, fill in ((id_f[:, :], 0, -1, ALU.not_equal, 1.0),
                                            (id_b[:, :], 0, -1, ALU.not_equal, 1.0),
                                            (flip, -(P - 1), 1, ALU.not_equal, 1.0)):
                g.affine_select(out=m, in_=m, pattern=[[step, P]], compare_op=op, fill=fill, base=base,
                                channel_multiplier=1).then_inc(cs, 1)
            g.affine_select(out=triT[:, :], in_=triT[:, :], pattern=[[1, P]], compare_op=ALU.is_ge,
                            fill=0.0, base=0, channel_multiplier=-1).then_inc(cs, 1)
            g.affine_select(out=causal[:, :], in_=causal[:, :], pattern=[[-1, P]], compare_op=ALU.is_ge,
                            fill=MASKED, base=0, channel_multiplier=1).then_inc(cs, 1)
            n = 21
            for m, s0, s1 in ((sel_s, (0, CI, 2 * CI), (SIDE0_ROWS, SIDE0_ROWS + CJ, SIDE0_ROWS + 2 * CJ)),
                              (sel_d, (3 * CI,), (SIDE0_ROWS + 3 * CJ,))):
                v = m[:, :].rearrange("r (j i) -> r j i", i=CI)
                for base, pat in [(s, [[0, CJ], [-1, CI]]) for s in s0] + [(s, [[-1, CJ], [0, CI]]) for s in s1]:
                    pool.wait_ge(cs, n)
                    g.affine_select(out=v, in_=v, pattern=pat, compare_op=ALU.not_equal, fill=1.0,
                                    base=-base, channel_multiplier=1).then_inc(cs, 1)
                    n += 1
            pool.wait_ge(S["ids_ok"], 1)
            for n in range(P // 4):
                wait(pool, S["emb_tr"], n - 3)
                for j in range(4):
                    g.indirect_dma_start(emb_t[:, n % 4, j, :], None, emb_table,
                                         bass.IndirectOffsetOnAxis(ids_u[:, 4 * n + j:4 * n + j + 1], 0)).then_inc(
                        S[f"emb_in{n % 4}"], 16)
            pool.wait_ge(S["buf_w"], 16)
            pool.wait_ge(S["span_ok"], 1)
            for r in range(ROUNDS):
                if r:
                    pool.wait_ge(S["scat_ok"], 128 * r)
                    pool.wait_ge(S["summed"], 4 * r)
                for m in range(8):
                    for s in range(SPAN):
                        g.indirect_dma_start(src_t[:, m, s, :], None, buf_d,
                                             bass.IndirectOffsetOnAxis(sp_u[:, r, m, s:s + 1], 0)).then_inc(
                            S[f"src_in{m // 4}"], 16)
                pool.wait_ge(S["dup_ok"], 1)
                for hf in range(2):
                    pool.wait_ge(S[f"src_in{hf}"], 16 * 16 * (r + 1))
                for m in range(8):
                    if m % 4 == 0:
                        pool.wait_ge(S["comp_ok"], 2 * r + m // 4 + 1)
                    g.indirect_dma_start(buf_d, bass.IndirectOffsetOnAxis(tg_u[:, r, m:m + 1], 0),
                                         comp_t[:, m, :], None, bounds_check=N_TOK - 1,
                                         oob_is_err=False).then_inc(S["scat_ok"], 16)

            def front(s, b):
                if s == 2:
                    pool.wait_ge(S["ve1_ok"], b + 1)
                    g.tensor_tensor(rstd[:, :], vareps[:, :], half[:, :], ALU.pow).then_inc(S["rstd1_ok"], 1)
                if s == 24:
                    pool.wait_ge(S["ve2_ok"], b + 1)
                    g.tensor_tensor(rstd[:, :], vareps[:, :], half[:, :], ALU.pow).then_inc(S["rstd2_ok"], 1)

            def tail(s, t):
                if s == 6:
                    pool.wait_ge(S["shift_ok"], t + 1)
                    wait(pool, S["low_ok"], 2 * t)
                    g.tensor_tensor(resid[:, 0], sim[:, 0], shift0[:, :, None].to_broadcast([P, HEADS, KEYS]),
                                    ALU.subtract).then_inc(S["shifted_ok"], 1)
                    g.tensor_tensor(resid[:, 1], sim[:, 1], top[:, 1, :, 0:1].to_broadcast([P, HEADS, KEYS]),
                                    ALU.subtract).then_inc(S["shifted_ok"], 1)
                if s in (10, 15):
                    if s == 10:
                        pool.wait_ge(S["high_ok"], 2 * (t + 1))
                    else:
                        pool.wait_ge(S["mid_ok"], 2 * (t + 1))
                    for side, pt in enumerate((parts0, parts1)):
                        v = resid[:, side].rearrange("p h (g i) -> p h g i", i=(CI, CJ)[side])
                        if s == 10:
                            g.tensor_tensor(v, v, pt[:, :, :, 0, :], ALU.subtract).then_inc(S["resid_ok"], 1)
                        else:
                            g.tensor_tensor(pt[:, :, :, 2, :], v, pt[:, :, :, 1, :], ALU.subtract).then_inc(
                                S["low_ok"], 1)
                if 5 <= s < 5 + HEADS:
                    h = s - 5
                    pool.wait_ge(S["hot0_ok"], HEADS * t + h + 1)
                    if h == 0:
                        pool.wait_ge(S["count_ok"], t + 1)
                    g.tensor_tensor(hot[:, 0, h], hot[:, 0, h],
                                    count[:, h, None, :].to_broadcast([P, KEYS, TOPK]), ALU.mult).then_inc(
                        S["weigh0_ok"], 1)
                if s in POOL_WEIGHS:
                    h = DVE_WEIGHS + POOL_WEIGHS.index(s)
                    pool.wait_ge(S["hot1_ok"], HEADS * t + h + 1)
                    g.tensor_tensor(hot[:, 1, h], hot[:, 1, h],
                                    rank_w[:, None, :].to_broadcast([P, KEYS, TOPK]), ALU.mult).then_inc(
                        S["weigh1_pool"], 1)

            def window(t, F, Tl, Bb, Cc, first=False, opening=False, last=False):
                for s in range(SLOTS):
                    if Tl:
                        tail(s, t)
                    if F:
                        front(s, t + 1)
            run_windows(pool, window)

        @block.tensor
        def _(pe):
            mm, tr = nc.tensor.matmul, nc.tensor.transpose

            def fence(column):
                mm(column, id_b[:, :], id_b[:, 0:1], start=True, stop=True)

            pe.wait_ge(S["consts"], 29)
            pe.wait_ge(S["loads_w"], 48)
            pe.wait_ge(S["loads_q"], 18 * 16)
            for k in range(4):
                tr(PS[0][:, k * C:(k + 1) * C], pkq[0:C, k * P:(k + 1) * P], id_f[0:C, 0:C])
                last = tr(PS[1][:, k * C:(k + 1) * C], keys_t[0:C, k * P:(k + 1) * P], id_f[0:C, 0:C])
            last.then_inc(S["pk_tr"], 1)
            pe.wait_ge(S["pk_c"], 2)
            for n in range(2 * HEADS):
                wait(pe, S["pk_step"], n)
                k, r = n // 4, (n % 4) * D_KEY
                last = mm(PD[n // HEADS][0:C, (n % HEADS) * KEYS:(n % HEADS + 1) * KEYS],
                          pkqT[r:r + D_KEY, k, :], keysT[r:r + D_KEY, k, :], start=True, stop=True)
                last.then_inc(S["pk_step"], 1)
            pe.wait_ge(S["tw_in"], 16)
            tr(PO[:, 0:P], toep_raw, id_f[:, :]).then_inc(S["toep_tr"], 1)
            pe.wait_ge(S["toep_c"], 1)
            mm(PO[:, P:2 * P], toep_mid, flip, start=True, stop=True).then_inc(S["toep_mm"], 1)
            with pe.Fori(0, P // 16) as i:
                for k in range(4):
                    n = 4 * i + k
                    pe.wait_ge(S[f"emb_in{k}"], 64 * (i + 1))
                    for j in range(4):
                        tr(PS[0][:, j * P:(j + 1) * P], emb_t[:, k, j, 0:P], id_f[:, :])
                        last = tr(PD[0][0:C, j * P:(j + 1) * P], emb_t[:, k, j, P:D_EMB], id_f[:, :])
                    last.then_inc(S["emb_tr"], 1)
                    pe.wait_ge(S["emb_c1"], n + 1)
                    pe.wait_ge(S["emb_c2"], n + 1)
                    for j in range(4):
                        mm(XA[:, j * C:(j + 1) * C], eT1[:, j * P:(j + 1) * P], wd1, start=True, stop=False)
                        last = mm(XA[:, j * C:(j + 1) * C], eT2[0:C + 1, j * P:(j + 1) * P],
                                  wd2[0:C + 1], start=False, stop=True)
                    last.then_inc(S["emb_mm"], 1)
                    pe.wait_ge(S["emb_out"], n + 1)
            pe.wait_ge(S["loads_p"], 64)
            pe.wait_ge(S["pk_ok"], 2)
            pe.wait_ge(S["toep_ok"], 1)
            for n in range(2 * ROUNDS):
                hf, first = n % 2, 4 * (n % 2)
                pe.wait_ge(S["mean_ok"], n + 1)
                for m in range(4):
                    last = tr((XA, XC)[hf][0:C, m * P:(m + 1) * P], mean_t[:, first + m, :], id_f[:, :])
                last.then_inc(S["mean_tr"], 1)
                pe.wait_ge(S["mean_c"], n + 1)
                for m in range(2):
                    mm((PS, PD)[m][hf][:, :], wc1_t[0:C + 1, m * P:(m + 1) * P],
                       meanT[0:C + 1, hf * 512:(hf + 1) * 512], start=True, stop=True).then_inc(S["hid_mm"], 1)
                pe.wait_ge(S["hid_ok"], 2 * (n + 1))
                wait(pe, S["comp_ok"], n)
                for m in range(first, first + 4):
                    o = XO[:, m * C:(m + 1) * C]
                    for k in range(2):
                        mm(o, hidT[:, k, m * P:(m + 1) * P], wc2_t[:, k, :], start=k == 0, stop=False)
                    last = mm(o, ones_r[0:1, :], bc2_t[0:1, :], start=False, stop=True)
                last.then_inc(S["comp_mm"], 1)
            pe.wait_ge(S["comp_ok"], 2 * ROUNDS)

            def chunk_scores(s, w):
                k, c, e = s // CHUNKS, s % CHUNKS, s % 2
                if c == 0:
                    pe.wait_ge(S[f"combo_in{k}"], LOAD_UNIT * (w + 1))
                wait(pe, S["exp_ready"], SLOTS * w + s - 1)
                mm(PS[e][:, :], sel_s[:, :], combo[0:ROWS, k, c, :], start=True, stop=True).then_inc(
                    S["scores_ready"], 1)

            def chunk_test(s, w):
                k, c = s // CHUNKS, s % CHUNKS
                wait(pe, S["weights_ready"], SLOTS * w + s - 1)
                mm(PD[s % 2][:, :], sel_d[:, :], combo[0:ROWS, k, c, :], start=True, stop=True).then_inc(
                    S["test_ready"], 1)

            def chunk_sum(s, w):
                w, s = (w, s) if s >= 0 else (w - 1, s + SLOTS)
                k, c = s // CHUNKS, s % CHUNKS
                if c == 0:
                    wait(pe, S["kv_ready"], 2 * w + k)
                pe.wait_ge(S["weights_ready"], SLOTS * w + s + 1)
                mm(PO[:, :], table[:, k, c, :], W[:, s % 4, :], start=c == 0, stop=c == CHUNKS - 1).then_inc(
                    S["pv_done"], 1)

            def front(s, b):
                if s == 5:
                    pe.wait_ge(S["xn2_ok"], b + 1)
                    wait(pe, S["sim1_ok"], b)
                    wait(pe, S["rows_c"], 4 * b - 4)
                    fence(XA[:, 0:1])
                    tr(XA[:, 0:P], xn2[:, :, :].rearrange("p a c -> p (a c)"), id_f[:, :]).then_inc(S["xn2_tr"], 1)
                if s == 7:
                    pe.wait_ge(S["xxT_ok"], 2 * (b + 1))
                    mm(XA[:, 0:3 * C], xxT[:, :], w_mix[:, :], start=True, stop=True).then_inc(S["kvr_mm"], 1)
                if s == 13:
                    pe.wait_ge(S["k_ok"], b + 1)
                    pe.wait_ge(S["kv_ok"], b + 1)
                    mm(XA[:, 192:256], triT[:, :], k_e[:, :], start=True, stop=True)
                    mm(XA[:, 256:320], toepT[:, :], kv_t[:, :], start=True, stop=True).then_inc(S["scan_mm"], 1)
                if s == 18:
                    pe.wait_ge(S["rwkv_ok"], b + 1)
                    fence(XA[:, 320:321])
                    tr(XA[0:C, 320:448], rwkv[:, :], id_f[:, :]).then_inc(S["rw_tr"], 1)
                if s == 20:
                    pe.wait_ge(S["rwT_ok"], b + 1)
                    fence(XA[:, 448:449])
                    mm(XA[:, 448:512], rwT[:, :], wo_a[:, :], start=True, stop=True).then_inc(S["proj_mm"], 1)
                if s == 27:
                    pe.wait_ge(S["xn_ok"], b + 1)
                    fence(XA[:, 0:1])
                    tr(XA[0:C, 0:P], xn[:, :], id_f[:, :]).then_inc(S["xn_tr"], 1)
                if s == 29:
                    pe.wait_ge(S["xnT_ok"], b + 1)
                    fence(XA[:, 0:1])
                    mm(XA[:, :], xnT[:, :], pk_m[:, 0:512], start=True, stop=True).then_inc(S["sim0_mm"], 1)
                if s == 31:
                    pe.wait_ge(S["sim0_ok"], b + 1)
                    fence(XA[:, 0:1])
                    mm(XA[:, :], xnT[:, :], pk_m[:, 512:1024], start=True, stop=True).then_inc(S["sim1_mm"], 1)

            def tail(s, t, F):
                if s in (34, 36, 38, 40):
                    n = (s - 34) // 2
                    if n == 0:
                        pe.wait_ge(S["tree0_step"], TREE * (t + 1))
                        pe.wait_ge(S["tree1_step"], TREE * (t + 1))
                        pe.wait_ge(S["low_ok"], 2 * (t + 1))
                        if F:
                            pe.wait_ge(S["sim1_ok"], t + 2)
                    else:
                        pe.wait_ge(S["rows_c"], 4 * t + n)
                    fence(XA[:, 0:1])
                    for j in range(8):
                        m = 8 * n + j
                        last = tr(XAb[:, j * P:(j + 1) * P], parts[:, m * P:(m + 1) * P], id_b[:, :])
                    last.then_inc(S["rows_tr"], 1)

            def attend(s, c):
                for hg, base in ((0, 38), (1, 50)):
                    n = 2 * c + hg
                    if s == base:
                        if hg == 0:
                            pe.wait_ge(S["c_in"], 48 * (c + 1))
                        wait(pe, S["attT_ok"], n)
                        fence(XC[:, 0:1])
                        for h in range(4):
                            last = mm(XC[0:C, h * T:(h + 1) * T], wq_t[:, (4 * hg + h) * C:(4 * hg + h + 1) * C],
                                      xnT_c[:, :], start=True, stop=True)
                        last.then_inc(S["q_mm"], 1)
                    if s == base + 2:
                        pe.wait_ge(S["q_ok"], n + 1)
                        wait(pe, S["vo_ok"], n)
                        wait(pe, S["res_ok"], n)
                        fence(XC[:, 0:1])
                        for h in range(4):
                            last = mm(XC[:, h * T:(h + 1) * T], qT[:, h, :], kv_c[0:C, 4 * hg + h, :],
                                      start=True, stop=True)
                        last.then_inc(S["att_mm"], 1)
                        for h in range(4):
                            last = mm(XO[:, h * C:(h + 1) * C], kv_c[C:P, 4 * hg + h, :], wo_f[C:P, 4 * hg + h, :],
                                      start=True, stop=True)
                        last.then_inc(S["vo_mm"], 1)
                    if s == base + 10:
                        pe.wait_ge(S["att_ok"], 4 * (n + 1))
                        fence(XC[:, 0:1])
                        for h in range(4):
                            last = tr(XC[:, h * T:(h + 1) * T], att[:, h, :], id_f[:, :])
                        last.then_inc(S["att_tr"], 1)
                    if s == base + 12:
                        pe.wait_ge(S["attT_ok"], n + 1)
                        pe.wait_ge(S["vo_ok"], n + 1)
                        fence(XO[:, 0:1])
                        for h in range(4):
                            last = mm(XO[:, 256:256 + C], attT[:, h, :], vo[:, h, :],
                                      start=h == 0, stop=h == 3)
                        last.then_inc(S["o_mm"], 1)

            def window(t, F, Tl, Bb, Cc, first=False, opening=False, last=False):
                w = t - 4
                for s in range(SLOTS):
                    if Bb:
                        chunk_test(s, w)
                        if s < SLOTS - 1:
                            chunk_scores(s + 1, w)
                        elif not last:
                            chunk_scores(0, w + 1)
                        if s % CHUNKS == 3:
                            chunk_sum(s - 3, w)
                        if s % CHUNKS != 2 and (s >= 2 or not opening):
                            chunk_sum(s - 2, w)
                    if F:
                        front(s, t + 1)
                    if Tl:
                        tail(s, t, F)
                    if Cc:
                        attend(s, t - 8)
                if first:
                    chunk_scores(0, w + 1)
                if last:
                    chunk_sum(SLOTS - 2, w)
                    chunk_sum(SLOTS - 1, w)
            run_windows(pe, window)

        @block.scalar
        def _(act):
            a = nc.scalar.activation
            act.wait_ge(S["pk_tr"], 1)
            a(pkqT, PS[0][:, 0:256].rearrange("p (k c) -> p k c", k=4), ACT.Copy).then_inc(S["pk_c"], 1)
            a(keysT, PS[1][:, 0:256].rearrange("p (k c) -> p k c", k=4), ACT.Copy).then_inc(S["pk_c"], 1)
            for n in range(2):
                act.wait_ge(S["pk_step"], HEADS * (n + 1))
                a(pk_m[:, n * 512:(n + 1) * 512], PD[n][0:C, :], ACT.Copy).then_inc(S["pk_ok"], 1)
            act.wait_ge(S["toep_tr"], 1)
            a(toep_mid, PO[:, 0:P], ACT.Copy).then_inc(S["toep_c"], 1)
            act.wait_ge(S["toep_mm"], 1)
            a(toepT[:, :], PO[:, P:2 * P], ACT.Copy).then_inc(S["toep_ok"], 1)
            with act.Fori(0, P // 16) as i:
                for k in range(4):
                    n = 4 * i + k
                    act.wait_ge(S["emb_tr"], n + 1)
                    a(eT1, PS[0][:, :], ACT.Copy).then_inc(S["emb_c1"], 1)
                    act.wait_ge(S["emb_mm"], n + 1)
                    a(rowbuf[:, bass.ds(n * 4 * C, 4 * C)], XA[:, 0:4 * C], ACT.Copy).then_inc(S["emb_out"], 1)
            for n in range(2 * ROUNDS):
                hf = n % 2
                act.wait_ge(S["mean_tr"], n + 1)
                a(meanT[0:C, hf * 512:(hf + 1) * 512], (XA, XC)[hf][0:C, :], ACT.Copy).then_inc(S["mean_c"], 1)
                for m in range(2):
                    act.wait_ge(S["hid_mm"], 2 * n + m + 1)
                    a(hidT[:, m, hf * 512:(hf + 1) * 512], (PS, PD)[m][hf][:, :], ACT.Gelu_apprx_tanh).then_inc(
                        S["hid_ok"], 1)

            def chunk_exp(s, w):
                act.wait_ge(S["scores_ready"], SLOTS * w + s + 1)
                wait(act, S["weights_ready"], SLOTS * w + s - 1)
                a(E[:, s % 2, :], PS[s % 2][:, :], ACT.Exp).then_inc(S["exp_ready"], 1)

            def unit_out(k, w):
                act.wait_ge(S["pv_done"], SLOTS * w + CHUNKS * (k + 1))
                wait(act, S[f"kv_w{k}"], 16 * w)
                a(kv_out[:, k, :], PO[:, :], ACT.Copy).then_inc(S["kv_ready"], 1)

            def front(s, b):
                if s == 6:
                    act.wait_ge(S["xn2_tr"], b + 1)
                    a(xxT[0:C, :], XA[0:C, 0:P], ACT.Copy).then_inc(S["xxT_ok"], 1)
                    a(xxT[C:P, 1:T], XA[C:P, 0:T - 1], ACT.Copy).then_inc(S["xxT_ok"], 1)
                if s == 10:
                    act.wait_ge(S["kclip_ok"], b + 1)
                    a(e_r[:, :], XA[:, 128:192], ACT.Exp, scale=-1.0).then_inc(S["er_ok"], 1)
                    a(k_e[:, :], k_c[:, :], ACT.Exp).then_inc(S["k_ok"], 1)
                if s == 19:
                    act.wait_ge(S["rw_tr"], b + 1)
                    a(rwT[:, :], XA[0:C, 320:448], ACT.Copy).then_inc(S["rwT_ok"], 1)
                if s == 28:
                    act.wait_ge(S["xn_tr"], b + 1)
                    wait(act, S["xn_w"], 16 * b)
                    a(xnT[:, :], XA[0:C, 0:P], ACT.Copy).then_inc(S["xnT_ok"], 1)
                for side, at in ((0, 30), (1, 32)):
                    if s == at:
                        act.wait_ge(S[f"sim{side}_mm"], b + 1)
                        wait(act, S["shifted_ok"], 2 * b)
                        a(sim[:, side], XA[:, :].rearrange("p (h k) -> p h k", h=HEADS), ACT.Copy).then_inc(
                            S[f"sim{side}_ok"], 1)
                if s == 53:
                    act.wait_ge(S["gap_ok"], b + 1)
                    a(expd[:, :, :], expd[:, :, :], ACT.Exp).then_inc(S["expd_ok"], 1)

            def tail(s, t):
                if s == 4:
                    act.wait_ge(S["z_ok"], t + 1)
                    a(lnz[:, :], zsum[:, :], ACT.Ln).then_inc(S["lnz_ok"], 1)
                if s in (10, 18):
                    if s == 10:
                        act.wait_ge(S["shifted_ok"], 2 * (t + 1))
                        wait(act, S["rows_tr"], 4 * t)
                    else:
                        act.wait_ge(S["resid_ok"], 2 * (t + 1))
                    part = (s - 10) // 8
                    for side, pt in enumerate((parts0, parts1)):
                        a(pt[:, :, :, part, :], resid[:, side].rearrange("p h (g i) -> p h g i", i=(CI, CJ)[side]),
                          ACT.Copy).then_inc(S[("high_ok", "mid_ok")[part]], 1)
                if s in (35, 37, 39, 41):
                    n = (s - 35) // 2
                    act.wait_ge(S["rows_tr"], 4 * t + n + 1)
                    if n == 0:
                        wait(act, S["rows_w"], 16 * t)
                    a(rowsT[:, n * 1024:(n + 1) * 1024], XAb[:, :], ACT.Copy).then_inc(S["rows_c"], 1)

            def attend(s, c):
                for hg, base in ((0, 38), (1, 50)):
                    n = 2 * c + hg
                    if s == base + 1:
                        act.wait_ge(S["q_mm"], n + 1)
                        a(qT[:, :, :], XC[0:C, :].rearrange("p (h t) -> p h t", h=4), ACT.Copy).then_inc(S["q_ok"], 1)
                    if s == base + 3:
                        act.wait_ge(S["vo_mm"], n + 1)
                        wait(act, S["o_mm"], n)
                        a(vo[:, :, :], XO[:, 0:256].rearrange("p (h d) -> p h d", h=4), ACT.Copy).then_inc(
                            S["vo_ok"], 1)
                    if s == base + 6:
                        act.wait_ge(S["nmax_ok"], n + 1)
                        for h in range(4):
                            a(att[:, h, :], att[:, h, :], ACT.Exp, bias=nmax[:, h:h + 1],
                              accum_out=asum[:, h:h + 1]).then_inc(S["aexp_ok"], 1)
                    if s == base + 9:
                        act.wait_ge(S["rsum_ok"], n + 1)
                        for h in range(4):
                            a(att[:, h, :], att[:, h, :], ACT.Copy, scale=rsum[:, h:h + 1]).then_inc(S["att_ok"], 1)
                    if s == base + 11:
                        act.wait_ge(S["att_tr"], n + 1)
                        a(attT[:, :, :], XC[:, :].rearrange("p (h t) -> p h t", h=4), ACT.Copy).then_inc(
                            S["attT_ok"], 1)

            def window(t, F, Tl, Bb, Cc, first=False, opening=False, last=False):
                w = t - 4
                for s in range(SLOTS):
                    if Bb:
                        chunk_exp(s, w)
                    if Bb and s == CHUNKS + 2:
                        unit_out(0, w)
                    if Bb and s == 2 and not opening:
                        unit_out(1, w - 1)
                    if F:
                        front(s, t + 1)
                    if Tl:
                        tail(s, t)
                    if Cc:
                        attend(s, t - 8)
                if last:
                    unit_out(1, w)
            run_windows(act, window)

        @block.vector
        def _(dve):
            v = nc.vector
            v.memset(fence_t[:, :], 0.0).then_inc(S["fence_v"], 1)
            dve.wait_ge(S["fence_v"], 1)

            def fence():
                v.tensor_copy(fence_t[:, 0:1], fence_t[:, 1:2])

            prep_n = [0]

            def step(ins):
                prep_n[0] += 1
                ins.then_inc(S["prep_step"], 1)
                dve.wait_ge(S["prep_step"], prep_n[0])

            def from_end(f, n, size):
                step(v.tensor_scalar(n, f, 0.0, float(size), ALU.is_lt, ALU.mult))
                step(v.tensor_tensor(f, f, n, ALU.add))

            dve.wait_ge(S["loads_x"], 16)
            step(v.tensor_copy(ids_f, ids_i))
            step(v.tensor_scalar(ids_n, ids_f, PAD, -PAD, ALU.is_equal, ALU.mult))
            step(v.tensor_tensor(ids_f, ids_f, ids_n, ALU.add))
            from_end(ids_f, ids_n, VOCAB)
            step(v.tensor_scalar(ids_f, ids_f, 0.0, VOCAB - 1.0, ALU.max, ALU.min))
            v.tensor_copy(ids_u, ids_f).then_inc(S["ids_ok"], 1)
            dve.wait_ge(S["loads_sp"], 48)
            step(v.tensor_copy(sp_f[:, :, :, :], sp_i[:, :, :, :]))
            step(v.tensor_reduce(tg_f[:, :, :], sp_f[:, :, :, :], AX.X, ALU.max))
            step(v.tensor_scalar(tg_f[:, :, :], tg_f[:, :, :], 1.0, None, ALU.add))
            from_end(tg_f[:, :, :], tg_n[:, :, :], N_TOK)
            step(v.tensor_scalar(tg_n[:, :, :], tg_f[:, :, :], 0.0, 1.0e6, ALU.is_lt, ALU.mult))
            v.tensor_tensor(tg_f[:, :, :], tg_f[:, :, :], tg_n[:, :, :], ALU.add).then_inc(S["sp_ok"], 1)
            step(v.tensor_scalar(sp_m[:, :, :, :], sp_f[:, :, :, :], PAD, None, ALU.not_equal))
            step(v.tensor_reduce(n_in[:, :, :], sp_m[:, :, :, :], AX.X, ALU.add))
            step(v.tensor_scalar(n_in[:, :, :], n_in[:, :, :], 1.0, None, ALU.max))
            step(v.reciprocal(n_in[:, :, :], n_in[:, :, :]))
            step(v.tensor_tensor(sp_f[:, :, :, :], sp_f[:, :, :, :], sp_m[:, :, :, :], ALU.mult))
            from_end(sp_f[:, :, :, :], sp_n[:, :, :, :], N_TOK)
            step(v.tensor_scalar(sp_f[:, :, :, :], sp_f[:, :, :, :], 0.0, N_TOK - 1.0, ALU.max, ALU.min))
            v.tensor_copy(sp_u[:, :, :, :], sp_f[:, :, :, :]).then_inc(S["span_ok"], 1)
            dve.wait_ge(S["consts"], 29)
            with dve.Fori(0, P // 16) as i:
                for k in range(4):
                    dve.wait_ge(S["emb_tr"], 4 * i + k + 1)
                    v.tensor_copy(eT2[0:C], PD[0][0:C, :]).then_inc(S["emb_c2"], 1)
            dve.wait_ge(S["loads_q"], 18 * 16)
            step(v.tensor_scalar(mixes[C:P, 0:3], mixes[C:P, 0:3], -1.0, 1.0, ALU.mult, ALU.add))
            for n in range(3):
                v.tensor_scalar(w_mix[:, n * C:(n + 1) * C], w_mix[:, n * C:(n + 1) * C], mixes[:, n:n + 1],
                                None, ALU.mult).then_inc(S["mix_ok"], 1)
            dve.wait_ge(S["tgt_in"], 48)
            for r in range(ROUNDS):
                for m in range(8):
                    step(v.tensor_scalar(same, tgt_row[:, r], tg_f[:, r, m:m + 1], None, ALU.is_equal))
                    step(v.scalar_tensor_tensor(junk, later, float(m), same, op0=ALU.is_gt, op1=ALU.mult,
                                                accum_out=dup[:, r, m:m + 1]))
            step(v.tensor_scalar(dup[:, :, :], dup[:, :, :], 0.0, 1.0e6, ALU.is_gt, ALU.mult))
            step(v.tensor_tensor(tg_f[:, :, :], tg_f[:, :, :], dup[:, :, :], ALU.add))
            v.tensor_copy(tg_u[:, :, :], tg_f[:, :, :]).then_inc(S["dup_ok"], 1)
            for n in range(2 * ROUNDS):
                r, hf = n // 2, n % 2
                g = slice(4 * hf, 4 * hf + 4)
                src, mean = src_t[:, g], mean_t[:, g]
                dve.wait_ge(S[f"src_in{hf}"], 16 * 16 * (r + 1))
                v.tensor_tensor(src, src, sp_m[:, r, g, :, None].to_broadcast([P, 4, SPAN, C]),
                                ALU.mult).then_inc(S["masked"], 1)
                dve.wait_ge(S["masked"], n + 1)
                v.tensor_tensor(src[:, :, 0:2], src[:, :, 0:2], src[:, :, 2:4], ALU.add).then_inc(S["summed"], 1)
                dve.wait_ge(S["summed"], 2 * n + 1)
                v.tensor_tensor(mean, src[:, :, 0], src[:, :, 1], ALU.add).then_inc(S["summed"], 1)
                dve.wait_ge(S["summed"], 2 * n + 2)
                v.tensor_tensor(mean, mean, n_in[:, r, g, None].to_broadcast([P, 4, C]), ALU.mult).then_inc(
                    S["mean_ok"], 1)
                dve.wait_ge(S["comp_mm"], n + 1)
                wait(dve, S["scat_ok"], 128 * r)
                v.tensor_copy(comp_t[:, g], XO[:, hf * 256:(hf + 1) * 256].rearrange(
                    "p (g d) -> p g d", g=4)).then_inc(S["comp_ok"], 1)

            def chunk_mask(s, w):
                dve.wait_ge(S["exp_ready"], SLOTS * w + s + 1)
                dve.wait_ge(S["test_ready"], SLOTS * w + s + 1)
                wait(dve, S["pv_done"], SLOTS * w + s - 3)
                v.scalar_tensor_tensor(W[:, s % 4, :], PD[s % 2][:, :], float(TOPK), E[:, s % 2, :],
                                       op0=ALU.is_gt, op1=ALU.mult).then_inc(S["weights_ready"], 1)

            def front(s, b):
                if s == 0:
                    dve.wait_ge(S["h0_in"], 16 * (b + 1))
                    v.bn_stats(stats[:, :], h0[:, :]).then_inc(S["stat1_ok"], 1)
                if s == 1:
                    dve.wait_ge(S["stat1_ok"], b + 1)
                    fence()
                    v.bn_aggr(mv[:, :], stats[:, :]).then_inc(S["var1_ok"], 1)
                    dve.wait_ge(S["var1_ok"], b + 1)
                    v.tensor_scalar(vareps[:, :], mv[:, 1:2], EPS, None, ALU.add).then_inc(S["ve1_ok"], 1)
                if s == 3:
                    dve.wait_ge(S["rstd1_ok"], b + 1)
                    wait(dve, S["xn2_tr"], b)
                    v.tensor_scalar(xn2[:, :, :], h0[:, None, :].to_broadcast([P, 2, C]), mv[:, 0:1], rstd[:, :],
                                    ALU.subtract, ALU.mult).then_inc(S["xn2_ok"], 1)
                if s == 8:
                    dve.wait_ge(S["kvr_mm"], b + 1)
                    v.tensor_scalar(k_c[:, :], XA[:, 0:C], -60.0, 30.0, ALU.max, ALU.min).then_inc(S["kclip_ok"], 1)
                if s == 11:
                    dve.wait_ge(S["k_ok"], b + 1)
                    v.tensor_tensor(kv_t[:, :], k_e[:, :], XA[:, C:2 * C], ALU.mult).then_inc(S["kv_ok"], 1)
                if s == 14:
                    dve.wait_ge(S["scan_mm"], b + 1)
                    dve.wait_ge(S["er_ok"], b + 1)
                    v.scalar_tensor_tensor(den[:, :], e_r[:, :], 1.0, XA[:, 192:256], op0=ALU.add,
                                           op1=ALU.mult).then_inc(S["den_ok"], 1)
                if s == 15:
                    dve.wait_ge(S["den_ok"], b + 1)
                    v.reciprocal(rden[:, :], den[:, :]).then_inc(S["rden_ok"], 1)
                if s == 16:
                    dve.wait_ge(S["rden_ok"], b + 1)
                    v.tensor_tensor(rwkv[:, :], rden[:, :], XA[:, 256:320], ALU.mult).then_inc(S["rwkv_ok"], 1)
                if s == 21:
                    dve.wait_ge(S["proj_mm"], b + 1)
                    wait(dve, S["h1_w"], 16 * b)
                    v.tensor_tensor(h1[:, :], h0[:, :], XA[:, 448:512], ALU.add).then_inc(S["h1_ok"], 1)
                if s == 22:
                    dve.wait_ge(S["h1_ok"], b + 1)
                    v.bn_stats(stats[:, :], h1[:, :]).then_inc(S["stat2_ok"], 1)
                if s == 23:
                    dve.wait_ge(S["stat2_ok"], b + 1)
                    fence()
                    v.bn_aggr(mv[:, :], stats[:, :]).then_inc(S["var2_ok"], 1)
                    dve.wait_ge(S["var2_ok"], b + 1)
                    v.tensor_scalar(vareps[:, :], mv[:, 1:2], EPS, None, ALU.add).then_inc(S["ve2_ok"], 1)
                if s == 25:
                    dve.wait_ge(S["rstd2_ok"], b + 1)
                    v.tensor_scalar(xn[:, :], h1[:, :], mv[:, 0:1], rstd[:, :], ALU.subtract, ALU.mult).then_inc(
                        S["xn_ok"], 1)
                if 31 <= s <= 49:
                    k = s - 31
                    if k == 0:
                        dve.wait_ge(S["sim0_ok"], b + 1)
                        wait(dve, S["shifted_ok"], 2 * b)
                    if k == 2:
                        dve.wait_ge(S["sim1_ok"], b + 1)
                    if k == 1:
                        wait(dve, S["low_ok"], 2 * b)
                    if k > 0:
                        dve.wait_ge(S["topk_step"], 19 * b + k)
                    fence()
                    for g, st in ((k - 3, 3), (k - 2, 2), (k - 1, 1), (k, 0)):
                        if not 0 <= g < 2 * HEADS:
                            continue
                        side, h = g // HEADS, g % HEADS
                        if st == 0:
                            last = v.max(top[:, side, h, 0:8], sim[:, side, h, :])
                        if st == 1:
                            v.max_index(idx[:, side, h, 0:8], top[:, side, h, 0:8], sim[:, side, h, :])
                            last = v.match_replace(simr[:, side, h, :], top[:, side, h, 0:8], sim[:, side, h, :], NEG)
                        if st == 2:
                            last = v.max(top[:, side, h, 8:16], simr[:, side, h, :])
                        if st == 3:
                            last = v.max_index(idx[:, side, h, 8:16], top[:, side, h, 8:16], simr[:, side, h, :])
                    last.then_inc(S["topk_step"], 1)
                if s in (49, 50):
                    v0, v1 = top[:, 0], top[:, 1]
                    if s == 49:
                        dve.wait_ge(S["topk_step"], 19 * (b + 1))
                        for r_ in range(3):
                            v.tensor_tensor(cand[:, :, STARTS[r_]:STARTS[r_] + RUNS[r_]],
                                            v0[:, :, r_:r_ + 1].to_broadcast([P, HEADS, RUNS[r_]]),
                                            v1[:, :, 0:RUNS[r_]], ALU.add)
                        v.tensor_copy(idx_b[:, :, :, :], idx[:, :, :, :]).then_inc(S["idxb_ok"], 1)
                    else:
                        for r_ in (3, 4):
                            v.tensor_tensor(cand[:, :, STARTS[r_]:STARTS[r_] + RUNS[r_]],
                                            v0[:, :, r_:r_ + 1].to_broadcast([P, HEADS, RUNS[r_]]),
                                            v1[:, :, 0:RUNS[r_]], ALU.add)
                        v.tensor_tensor(cand[:, :, STARTS[5]:STARTS[8]].rearrange("p h (a b) -> p h a b", b=2),
                                        v0[:, :, 5:8, None].to_broadcast([P, HEADS, 3, 2]),
                                        v1[:, :, None, 0:2].to_broadcast([P, HEADS, 3, 2]), ALU.add)
                        v.tensor_tensor(cand[:, :, STARTS[8]:], v0[:, :, 8:16],
                                        v1[:, :, 0:1].to_broadcast([P, HEADS, 8]), ALU.add).then_inc(S["cand_ok"], 1)
                if 51 <= s <= 61:
                    k = s - 51
                    if k == 0:
                        dve.wait_ge(S["cand_ok"], b + 1)
                        v.tensor_tensor(expd[:, :, :], cand[:, :, :], cand[:, :, 0:1].to_broadcast([P, HEADS, PAIRS]),
                                        ALU.subtract).then_inc(S["gap_ok"], 1)
                    else:
                        dve.wait_ge(S["stair_step"], 11 * b + k)
                        fence()
                    for h, st in ((k - 3, 3), (k - 2, 2), (k - 1, 1), (k, 0)):
                        if not 0 <= h < HEADS:
                            continue
                        if st == 0:
                            last = v.max(top_a[:, h, :], cand[:, h, :])
                        if st == 1:
                            last = v.match_replace(candr[:, h, :], top_a[:, h, :], cand[:, h, :], NEG)
                        if st == 2:
                            last = v.max(top_b[:, h, :], candr[:, h, :])
                        if st == 3:
                            last = v.match_replace(picked[:, h, :], top_b[:, h, :], candr[:, h, :], NEG)
                    last.then_inc(S["stair_step"], 1)
                if s == 62:
                    dve.wait_ge(S["stair_step"], 11 * (b + 1))
                    v.tensor_scalar(picked[:, :, :], picked[:, :, :], NEG / 2, None, ALU.is_lt).then_inc(
                        S["picked_ok"], 1)
                if s == 63:
                    dve.wait_ge(S["picked_ok"], b + 1)
                    dve.wait_ge(S["expd_ok"], b + 1)
                    v.tensor_tensor(expd[:, :, :], expd[:, :, :], picked[:, :, :], ALU.mult).then_inc(
                        S["weighed_ok"], 1)

            def tail(s, t):
                if s == 1:
                    dve.wait_ge(S["weighed_ok"], t + 1)
                    v.tensor_reduce(zsum[:, :], expd[:, :, :], AX.X, ALU.add).then_inc(S["z_ok"], 1)
                with nc.allow_low_precision(reason="counts up to 16 are exact in bf16"):
                    if s == 2:
                        for r_ in range(3):
                            v.tensor_reduce(count[:, :, r_:r_ + 1], picked[:, :, STARTS[r_]:STARTS[r_] + RUNS[r_]],
                                            AX.X, ALU.add)
                    if s == 3:
                        for r_ in (3, 4):
                            v.tensor_reduce(count[:, :, r_:r_ + 1], picked[:, :, STARTS[r_]:STARTS[r_] + RUNS[r_]],
                                            AX.X, ALU.add)
                        v.tensor_reduce(count[:, :, 5:8], picked[:, :, STARTS[5]:STARTS[8]].rearrange(
                            "p h (a b) -> p h a b", b=2), AX.X, ALU.add)
                        v.tensor_copy(count[:, :, 8:16], picked[:, :, STARTS[8]:]).then_inc(S["count_ok"], 1)
                if s == 5:
                    dve.wait_ge(S["lnz_ok"], t + 1)
                    v.tensor_tensor(shift0[:, :], top[:, 0, :, 0], lnz[:, :], ALU.add).then_inc(S["shift_ok"], 1)
                for m in range(2 * HEADS):
                    if s != HOT_SLOTS[m]:
                        continue
                    side, h = m // HEADS, m % HEADS
                    if m == 0:
                        dve.wait_ge(S["idxb_ok"], t + 1)
                        wait(dve, S["tree0_step"], TREE * t)
                    v.tensor_tensor(hot[:, side, h], idx_b[:, side, h, None, :].to_broadcast(
                        [P, KEYS, TOPK]), key_no[:, :, :], ALU.is_equal).then_inc(S[f"hot{side}_ok"], 1)
                if 16 <= s < 16 + DVE_WEIGHS:
                    h = s - 16
                    dve.wait_ge(S["hot1_ok"], HEADS * t + h + 1)
                    v.tensor_tensor(hot[:, 1, h], hot[:, 1, h],
                                    rank_w[:, None, :].to_broadcast([P, KEYS, TOPK]), ALU.mult).then_inc(
                        S["weigh1_ok"], 1)
                for side, at in TREE_SLOTS.get(s, ()):
                    st = S[f"tree{side}_step"]
                    if at < 4:
                        if side == 0:
                            dve.wait_ge(S["weigh0_ok"], HEADS * t + 2 * at + 2)
                        elif 2 * at < DVE_WEIGHS:
                            dve.wait_ge(S["weigh1_ok"], DVE_WEIGHS * t + 2 * at + 2)
                        else:
                            dve.wait_ge(S["weigh1_pool"], (HEADS - DVE_WEIGHS) * t + 2 * at + 2 - DVE_WEIGHS)
                        x_ = hot[:, side, 2 * at:2 * at + 2]
                        v.tensor_tensor(x_[:, :, :, 0:8], x_[:, :, :, 0:8], x_[:, :, :, 8:16], ALU.add).then_inc(st, 1)
                    elif at < 6:
                        n = (4, 2)[at - 4]
                        dve.wait_ge(st, TREE * t + at)
                        x_ = hot[:, side]
                        v.tensor_tensor(x_[:, :, :, 0:n], x_[:, :, :, 0:n], x_[:, :, :, n:2 * n],
                                        ALU.add).then_inc(st, 1)
                    else:
                        dve.wait_ge(st, TREE * t + at)
                        wait(dve, S["rows_tr"], 4 * t)
                        pt, n = ((parts0, CI), (parts1, CJ))[side]
                        x_ = hot[:, side].rearrange("p h (g i) a -> p h g i a", i=n)
                        v.tensor_tensor(pt[:, :, :, 3, :], x_[:, :, :, :, 0], x_[:, :, :, :, 1],
                                        ALU.add).then_inc(st, 1)

            def attend(s, c):
                for hg, base in ((0, 38), (1, 50)):
                    n = 2 * c + hg
                    if s == base + 3:
                        dve.wait_ge(S["att_mm"], n + 1)
                        wait(dve, S["att_tr"], n)
                        v.scalar_tensor_tensor(att[:, :, :], XC[:, :].rearrange("p (h t) -> p h t", h=4), C ** -0.5,
                                               causal[:, None, :].to_broadcast([P, 4, T]), op0=ALU.mult,
                                               op1=ALU.add).then_inc(S["masked_ok"], 1)
                    if s == base + 4:
                        dve.wait_ge(S["masked_ok"], n + 1)
                        v.tensor_reduce(nmax[:, :], att[:, :, :], AX.X, ALU.max, negate=True).then_inc(
                            S["nmax_ok"], 1)
                    if s == base + 7:
                        dve.wait_ge(S["aexp_ok"], 4 * (n + 1))
                        v.reciprocal(rsum[:, :], asum[:, :]).then_inc(S["rsum_ok"], 1)
                    if s == base + 13:
                        dve.wait_ge(S["o_mm"], n + 1)
                        if hg == 0:
                            wait(dve, S["out_w"], 16 * c)
                        else:
                            dve.wait_ge(S["res_ok"], n)
                        v.tensor_tensor(res[:, :], (h1_c, res)[hg][:, :], XO[:, 256:256 + C], ALU.add).then_inc(
                            S["res_ok"], 1)

            def window(t, F, Tl, Bb, Cc, first=False, opening=False, last=False):
                w = t - 4
                for s in range(SLOTS):
                    if Bb:
                        chunk_mask(s, w)
                    if F:
                        front(s, t + 1)
                    if Tl:
                        tail(s, t)
                    if Cc:
                        attend(s, t - 8)
            run_windows(dve, window)


def run_windows(eng, window):
    window(-1, True, False, False, False)
    window(0, True, True, False, False)
    with eng.Fori(1, 3) as t:
        window(t, True, True, False, False)
    window(3, True, True, False, False, first=True)
    window(4, True, True, True, False, opening=True)
    window(5, True, True, True, False)
    with eng.Fori(6, 8) as t:
        window(t, True, True, True, False)
    window(8, True, True, True, True)
    with eng.Fori(4, B // 2 - 1) as i:
        window(2 * i + 1, True, True, True, True)
        window(2 * i + 2, True, True, True, True)
    window(B - 1, False, True, True, True)
    with eng.Fori(B, B + 3) as t:
        window(t, False, False, True, True)
    window(B + 3, False, False, True, True, last=True)
    with eng.Fori(B + 4, B + 8) as t:
        window(t, False, False, False, True)


_INS = ["x", "L0_tok_spans0", "L0_tok_spans1", "L0_tok_spans2", "L0_tok_emb_table", "L0_tok_w_down",
        "L0_tok_b_down", "L0_tok_wc1", "L0_tok_bc1", "L0_tok_wc2", "L0_tok_bc2", "L0_attn_time_w",
        "L0_attn_time_mix_k", "L0_attn_time_mix_v", "L0_attn_time_mix_r", "L0_attn_Wk", "L0_attn_Wv",
        "L0_attn_Wr", "L0_attn_Wo", "L0_ffn_Wq_pk", "L0_ffn_pk_keys", "L0_ffn_Wq", "L0_ffn_keys_table",
        "L0_ffn_values_table", "L0_ffn_Wo"]


def kernel(**inputs):
    import concourse.bacc as bacc
    from concourse.bass_utils import run_bass_kernel_spmd
    arrays = {f"in_{n}": np.ascontiguousarray(inputs[n]) for n in _INS}
    nc = bacc.Bacc("TRN2", target_bir_lowering=False, num_devices=1)
    args = [nc.dram_tensor(f"in_{n}", arrays[f"in_{n}"].shape, mybir.dt.from_np(arrays[f"in_{n}"].dtype),
                           kind="ExternalInput").ap() for n in _INS]
    out = nc.dram_tensor("out_h", (B, T, C), F32, kind="ExternalOutput").ap()
    tower(nc, *args, out)
    r = run_bass_kernel_spmd(nc, [arrays], core_ids=[0])
    return r.results[0]["out_h"]
```
